# Optimizing a Trainium2 kernel written in Bass

```python
import numpy as np
import jax
import jax.numpy as jnp

def _softmax(x, axis=-1):
    return jax.nn.softmax(x, axis=axis)

def _gelu(x):
    return jax.nn.gelu(x, approximate=True)

def _silu(x):
    return jax.nn.silu(x)

def _sigmoid(x):
    return jax.nn.sigmoid(x)

def _layernorm(x, axis=-1, eps=1e-05):
    m = jnp.mean(x, axis=axis, keepdims=True)
    v = jnp.var(x, axis=axis, keepdims=True)
    return (x - m) / jnp.sqrt(v + eps)

def _scatter_add(tgt, idx, src, axis=0):
    return tgt.at[idx].add(src)

def _segment_sum(src, seg, n):
    return jax.ops.segment_sum(src, seg, n)
kernel_name = 'mk_macaron_d1_jaxref_r8_653b6c'

def setup_inputs(seed: int=0):
    np.random.seed(seed)
    _w = jnp.asarray

    def _L0_attn_setup():
        import jax, jax.numpy as jnp
        import numpy as np
        DECAY_CONSTANT = 1.0

        def _build_decay_matrices(weight, decay_value, S, dtype):
            i = jnp.arange(S)[:, None]
            j = jnp.arange(S)[None, :]
            mask = j >= i
            e = jnp.where(mask, (j - i).astype(dtype), jnp.asarray(0.0, dtype))
            dv0 = jnp.clip(decay_value[0, 0], 0.9, 1.0).astype(dtype)
            dv1 = jnp.clip(decay_value[1, 0], 0.9, 1.0).astype(dtype)
            w0 = weight[0].astype(dtype)
            w1 = weight[1].astype(dtype)
            Wr = jnp.where(mask, w0[:, None] * (dv0 ** e / DECAY_CONSTANT), jnp.asarray(0.0, dtype))
            Wc = jnp.where(mask, w1[None, :] * dv1 ** (e / DECAY_CONSTANT), jnp.asarray(0.0, dtype))
            return (Wr, Wc)
        key = jax.random.key(seed)
        kx, kw = jax.random.split(key)
        B, E, S = (4, 256, 256)
        x = jax.random.normal(kx, (B, E, S), dtype=jnp.float32)
        weight = jax.random.normal(kw, (2, S), dtype=jnp.float32)
        bias = jnp.zeros((S,), dtype=jnp.float32)
        decay_value = jnp.ones((2, 1), dtype=jnp.float32)
        return {'x': x, 'weight': weight, 'bias': bias, 'decay_value': decay_value}
    _L0_attn_in = _L0_attn_setup()

    def _L0_ffn_setup():
        import jax, jax.numpy as jnp
        import numpy as np
        HIDDEN = 256
        INTER = 1024
        SCALE = 64.0

        def fwht(x):
            orig_shape = x.shape
            n = orig_shape[-1]
            x = x.reshape(-1, n)
            h = 1
            while h < n:
                x = x.reshape(-1, n // (2 * h), 2, h)
                a, b = (x[:, :, 0, :], x[:, :, 1, :])
                x = jnp.stack([a + b, a - b], axis=2).reshape(-1, n)
                h *= 2
            return (x / jnp.sqrt(jnp.asarray(n, x.dtype))).reshape(orig_shape)
        key = jax.random.key(seed)
        ks = jax.random.split(key, 8)
        inp = jax.random.normal(ks[0], (4, 256, HIDDEN), dtype=jnp.float32)
        SU_ug = jnp.where(jax.random.bernoulli(ks[1], 0.5, (HIDDEN,)), 1.0, -1.0).astype(jnp.float32)
        SU_dp = jnp.where(jax.random.bernoulli(ks[2], 0.5, (INTER,)), 1.0, -1.0).astype(jnp.float32)
        Wscale_ug = jax.random.uniform(ks[3], (2 * INTER,), jnp.float32, 0.5, 1.5)
        Wscale_dp = jax.random.uniform(ks[4], (HIDDEN,), jnp.float32, 0.5, 1.5)
        W_up = jax.random.normal(ks[5], (INTER, HIDDEN), dtype=jnp.float32) * 0.02
        W_gate = jax.random.normal(ks[6], (INTER, HIDDEN), dtype=jnp.float32) * 0.02
        W_down = jax.random.normal(ks[7], (HIDDEN, INTER), dtype=jnp.float32) * 0.02
        return {'input': inp, 'SU_ug': SU_ug, 'SU_dp': SU_dp, 'Wscale_ug': Wscale_ug, 'Wscale_dp': Wscale_dp, 'W_up': W_up, 'W_gate': W_gate, 'W_down': W_down}
    _L0_ffn_in = _L0_ffn_setup()
    _d = {'L0_attn_x': _L0_attn_in['x'], 'L0_attn_weight': _L0_attn_in['weight'], 'L0_attn_bias': _L0_attn_in['bias'], 'L0_attn_decay_value': _L0_attn_in['decay_value'], 'L0_ffn_SU_ug': _L0_ffn_in['SU_ug'], 'L0_ffn_SU_dp': _L0_ffn_in['SU_dp'], 'L0_ffn_Wscale_ug': _L0_ffn_in['Wscale_ug'], 'L0_ffn_Wscale_dp': _L0_ffn_in['Wscale_dp'], 'L0_ffn_W_up': _L0_ffn_in['W_up'], 'L0_ffn_W_gate': _L0_ffn_in['W_gate'], 'L0_ffn_W_down': _L0_ffn_in['W_down']}
    _x0 = _d['L0_attn_x']
    _d['L0_attn_x'] = jax.random.normal(jax.random.fold_in(jax.random.key(seed), 1), (16, 256, 256), dtype=_x0.dtype)
    del _x0
    return _d

def reference(L0_attn_x, L0_attn_weight, L0_attn_bias, L0_attn_decay_value, L0_ffn_SU_ug, L0_ffn_SU_dp, L0_ffn_Wscale_ug, L0_ffn_Wscale_dp, L0_ffn_W_up, L0_ffn_W_gate, L0_ffn_W_down):

    def _L0_attn_ref(x, weight, bias, decay_value):
        import jax, jax.numpy as jnp
        import numpy as np
        DECAY_CONSTANT = 1.0

        def _build_decay_matrices(weight, decay_value, S, dtype):
            i = jnp.arange(S)[:, None]
            j = jnp.arange(S)[None, :]
            mask = j >= i
            e = jnp.where(mask, (j - i).astype(dtype), jnp.asarray(0.0, dtype))
            dv0 = jnp.clip(decay_value[0, 0], 0.9, 1.0).astype(dtype)
            dv1 = jnp.clip(decay_value[1, 0], 0.9, 1.0).astype(dtype)
            w0 = weight[0].astype(dtype)
            w1 = weight[1].astype(dtype)
            Wr = jnp.where(mask, w0[:, None] * (dv0 ** e / DECAY_CONSTANT), jnp.asarray(0.0, dtype))
            Wc = jnp.where(mask, w1[None, :] * dv1 ** (e / DECAY_CONSTANT), jnp.asarray(0.0, dtype))
            return (Wr, Wc)
        B, E, S = x.shape
        Wr, Wc = _build_decay_matrices(weight, decay_value, S, x.dtype)
        out = jnp.einsum('bes,st->bet', x, Wr + Wc)
        out = out + bias.astype(x.dtype)
        return out

    def _L0_ffn_ref(input, SU_ug, SU_dp, Wscale_ug, Wscale_dp, W_up, W_gate, W_down):
        import jax, jax.numpy as jnp
        import numpy as np
        HIDDEN = 256
        INTER = 1024
        SCALE = 64.0

        def fwht(x):
            orig_shape = x.shape
            n = orig_shape[-1]
            x = x.reshape(-1, n)
            h = 1
            while h < n:
                x = x.reshape(-1, n // (2 * h), 2, h)
                a, b = (x[:, :, 0, :], x[:, :, 1, :])
                x = jnp.stack([a + b, a - b], axis=2).reshape(-1, n)
                h *= 2
            return (x / jnp.sqrt(jnp.asarray(n, x.dtype))).reshape(orig_shape)
        n = SU_ug.shape[0]
        x = input.reshape(-1, n)
        x = fwht(x * SU_ug) / SCALE
        x_up = x @ W_up.T * (Wscale_ug[:INTER] * SCALE)
        x_gate = x @ W_gate.T * (Wscale_ug[INTER:] * SCALE)
        x = jax.nn.silu(x_gate) * x_up
        x = fwht(x * SU_dp) / SCALE
        x = x @ W_down.T * (Wscale_dp * SCALE)
        return x.reshape(input.shape)
    x = L0_attn_x
    x = x + 0.5 * _L0_ffn_ref(_layernorm(x, axis=-1), L0_ffn_SU_ug, L0_ffn_SU_dp, L0_ffn_Wscale_ug, L0_ffn_Wscale_dp, L0_ffn_W_up, L0_ffn_W_gate, L0_ffn_W_down)
    x = x + _L0_attn_ref(_layernorm(x, axis=-1), L0_attn_weight, L0_attn_bias, L0_attn_decay_value)
    x = x + 0.5 * _L0_ffn_ref(_layernorm(x, axis=-1), L0_ffn_SU_ug, L0_ffn_SU_dp, L0_ffn_Wscale_ug, L0_ffn_Wscale_dp, L0_ffn_W_up, L0_ffn_W_gate, L0_ffn_W_down)
    return x

_drawn_inputs = setup_inputs


def setup_inputs(seed=0):
    import zlib

    import numpy as np

    out = dict(_drawn_inputs(seed))
    spreads = {'L0_attn_bias': (0.0, 2.0), 'L0_attn_decay_value': (1.0, 0.6)}
    factors = {'L0_ffn_SU_ug': 2.94,
     'L0_ffn_SU_dp': 2.881,
     'L0_ffn_Wscale_ug': 7.558,
     'L0_ffn_Wscale_dp': 8.0,
     'L0_ffn_W_up': 2.926,
     'L0_ffn_W_gate': 2.963,
     'L0_ffn_W_down': 2.927,
     'L0_attn_weight': 64.0}
    for name, (base, spread) in spreads.items():
        noise = np.random.default_rng([zlib.crc32(name.encode()), seed]).standard_normal(out[name].shape)
        drawn = base * np.exp(spread * noise) if base else spread * noise
        out[name] = jnp.asarray(drawn.astype(out[name].dtype))
    for name, factor in factors.items():
        out[name] = (out[name] * factor).astype(out[name].dtype)
    return out
```

```python
from contextlib import ExitStack

import concourse.bass as bass
from concourse import mybir

ALU = mybir.AluOpType
ACT = mybir.ActivationFunctionType
F32 = mybir.dt.float32
F16 = mybir.dt.float16
I32 = mybir.dt.int32
AX_X = mybir.AxisListType.X
ABSMAX = bass.bass_isa.ReduceOp.absmax

P = 128
EPS = 1e-5
TINY = 1e-30

XS = 2.0 ** 10
WS = 2.0 ** 7
F16_TOP = 2.0 ** 15
MIX_TOP = 2.0 ** 14

HI, LO = 0, 1
UP, GATE = 0, 1


def macaron_kernel(nc, x, mix_w, mix_b, decay, su_ug, su_dp, ws_ug, ws_dp, w_up, w_gate, w_down, out):
    B, E, D = x.shape
    INTER = w_up.shape[0]
    TT = 4
    SLOT = TT * P
    NIT = B * E // (2 * SLOT)
    KB = D // P
    NC = INTER // P
    NG = 4
    JOBS = 4
    LNS = 6
    MIXS = 2
    LAG = 2

    PLAN = [(0, "load"), (1, "mix"), (0, "mix"), (1, "load")]
    LN_FIRST = [1, 2, 4, 6]

    x_d = x.rearrange("b e d -> (b e) d").rearrange("(g p t) d -> g p t d", p=P, t=TT)
    out_d = out.rearrange("b e d -> (b e) d").rearrange("(g p t) d -> g p t d", p=P, t=TT)
    w_d = {UP: w_up.rearrange("(m p) d -> p m d", p=P), GATE: w_gate.rearrange("(m p) d -> p m d", p=P)}
    wd_d = w_down.rearrange("(b p) n -> p b n", p=P)

    ctx = ExitStack()
    with ctx:
        def sb(name, shape, dt=F32):
            return ctx.enter_context(nc.sbuf_tensor(name, shape, dt))

        def sem(name):
            return ctx.enter_context(nc.semaphore(name))

        xs = sb("xs", [P, 2, TT, D])
        xn = sb("xn", [P, TT, D])
        xT = sb("xT", [P, 2, 2, KB, SLOT], F16)
        act = sb("act", [P, NC, 2, SLOT], F16)
        sil = sb("sil", [P, 2, SLOT])
        a32 = sb("a32", [P, 2, SLOT])
        wug = sb("wug", [P, 2, 2, KB, INTER], F16)
        wdn = sb("wdn", [P, NC, 2, D], F16)
        wmix = sb("wmix", [P, 2, D + P], F16)
        bias = sb("bias", [P, D])
        stats = sb("stats", [P, TT, 6])
        mv = sb("mv", [P, TT, 2])
        ve = sb("ve", [P, TT])
        nmean = sb("nmean", [P, TT])
        rstd = sb("rstd", [P, TT])
        nmr = sb("nmr", [P, TT])
        mhalf = sb("mhalf", [P, TT])
        mone = sb("mone", [P, TT])
        eps = sb("eps", [P, TT])
        wn = sb("wn", [P, 2, NC, D])
        wds = sb("wds", [P, 2, 2, NC, P])
        wTa = sb("wTa", [P, 2, SLOT])
        bfl = sb("bfl", [P, 2, 2, SLOT])
        wdT = sb("wdT", [P, 2, SLOT])
        rowi = sb("rowi", [P, P], I32)
        coli = sb("coli", [P, P], I32)
        par = sb("par", [P, P], I32)
        part = sb("part", [P, P], I32)
        had = sb("had", [P, P])
        ident = sb("ident", [P, P])
        NROWS = 2 * NC + KB + NC + KB + KB
        rows = sb("rows", [NROWS, P])
        cols = sb("cols", [P, NROWS])
        su_bc = sb("su_bc", [P, D])
        mix_bc = sb("mix_bc", [P, 2, D])
        dec_bc = sb("dec_bc", [P, 2])
        rmax = sb("rmax", [P, 2 * NC])
        rinv = sb("rinv", [P, 2 * NC])
        sumx = sb("sumx", [P, 1])
        suinv = sb("suinv", [P, 1])
        sk = sb("sk", [P, KB])
        sug = sb("sug", [P, 2 * NC])
        asg = sb("asg", [P, NC])
        asgi = sb("asgi", [P, NC])
        beta = sb("beta", [P, NC])
        fch = sb("fch", [P, NC])
        feta = sb("feta", [P, NC])
        mx = sb("mx", [P, 2])
        mxg = sb("mxg", [P, 2])
        fall = sb("fall", [P, 1])
        finv = sb("finv", [P, 1])
        kdown = sb("kdown", [P, 1])
        pw = sb("pw", [P, 9, 2])
        rp = sb("rp", [P, 2, D])
        dg = sb("dg", [P, 2, P])
        rpd = sb("rpd", [P, 2])
        rpi = sb("rpi", [P, 2])
        mmx = sb("mmx", [P, 2])
        msum = sb("msum", [P, 1])
        minv = sb("minv", [P, 1])
        kmix = sb("kmix", [P, 1])
        w0s = sb("w0s", [P, KB])
        mxa = sb("mxa", [P, D + P])
        mxb = sb("mxb", [P, D + P])
        mxc = sb("mxc", [P, D + P])

        C_WS = slice(0, 2 * NC)
        C_SUG = slice(2 * NC, 2 * NC + KB)
        C_SUD = slice(2 * NC + KB, 3 * NC + KB)
        C_WSD = slice(3 * NC + KB, 3 * NC + 2 * KB)
        C_W0 = slice(3 * NC + 2 * KB, 3 * NC + 3 * KB)

        G = [ctx.enter_context(nc.psum_tensor(f"G{i}", [P, 512], F32)) for i in range(2)]
        U = [ctx.enter_context(nc.psum_tensor(f"U{i}", [P, 512], F32)) for i in range(2)]
        Dn = [ctx.enter_context(nc.psum_tensor(f"Dn{i}", [P, 512], F32)) for i in range(2)]
        T = [ctx.enter_context(nc.psum_tensor(f"T{i}", [P, 512], F32)) for i in range(2)]
        TP = [T, Dn]
        HP = [G, U]

        wn_in = [sem(f"wn_in{q}") for q in range(NG)]
        wd_in = sem("wd_in")
        rows_in = sem("rows_in")
        bc_in = sem("bc_in")
        x_in = [sem("x_in0"), sem("x_in1")]
        x_out = [sem("x_out0"), sem("x_out1")]
        iotas = sem("iotas")
        consts = sem("consts")
        had_ready = sem("had_ready")
        ident_ready = sem("ident_ready")
        rows_T = sem("rows_T")
        cols_ready = sem("cols_ready")
        sk_ready = sem("sk_ready")
        rinv_ready = sem("rinv_ready")
        w_scaled = sem("w_scaled")
        w_T = sem("w_T")
        wTa_ready = sem("wTa_ready")
        bfl_ready = sem("bfl_ready")
        w_fold = sem("w_fold")
        whi_ready = sem("whi_ready")
        wlo_ready = sem("wlo_ready")
        mx_ready = sem("mx_ready")
        mxg_ready = sem("mxg_ready")
        wd_scaled = sem("wd_scaled")
        wd_bfl = sem("wd_bfl")
        wd_T = sem("wd_T")
        wdT_ready = sem("wdT_ready")
        wd_fold = sem("wd_fold")
        feta_ready = sem("feta_ready")
        wdhi_ready = sem("wdhi_ready")
        wdlo_ready = sem("wdlo_ready")
        scales_ready = sem("scales_ready")
        mixk_ready = sem("mixk_ready")
        mix_chain = sem("mix_chain")
        wmix_ready = sem("wmix_ready")
        dve_chain = sem("dve_chain")

        gate_done = sem("gate_done")
        up_done = sem("up_done")
        down_done = sem("down_done")
        tr_done = sem("tr_done")
        mix_done = sem("mix_done")
        silu_ready = sem("silu_ready")
        ahi_ready = sem("ahi_ready")
        xn_ready = sem("xn_ready")
        xThi_ready = sem("xThi_ready")
        a32_ready = sem("a32_ready")
        alo_ready = sem("alo_ready")
        x_ffn = sem("x_ffn")
        x_mix = sem("x_mix")
        stats_ready = sem("stats_ready")
        mv_ready = sem("mv_ready")
        xTlo_ready = sem("xTlo_ready")
        ln_small = sem("ln_small")
        bias_added = sem("bias_added")

        block = ctx.enter_context(nc.Block())

        @block.sync
        def _(sp):
            sp.dma_start(rows[0:2 * NC, :], ws_ug.rearrange("(r c) -> r c", c=P)).then_inc(rows_in, 16)
            sp.dma_start(rows[C_SUG, :], su_ug.rearrange("(r c) -> r c", c=P)).then_inc(rows_in, 16)
            sp.dma_start(rows[C_SUD, :], su_dp.rearrange("(r c) -> r c", c=P)).then_inc(rows_in, 16)
            sp.dma_start(rows[C_WSD, :], ws_dp.rearrange("(r c) -> r c", c=P)).then_inc(rows_in, 16)
            sp.dma_start(rows[C_W0, :], mix_w[0:1, :].rearrange("a (r c) -> (a r) c", c=P)).then_inc(rows_in, 16)
            for q in range(NG):
                half, kind = divmod(q, 2)
                sp.dma_start(wn[:, kind, 4 * half:4 * half + 4, :],
                             w_d[kind][:, 4 * half:4 * half + 4, :]).then_inc(wn_in[q], 16)
                if q == 1:
                    sp.dma_start(xs[:, 0, :, :], x_d[0]).then_inc(x_in[0], 16)
            sp.dma_start(wds[:, 0, :, :, :].rearrange("p b c k -> p b (c k)"), wd_d).then_inc(wd_in, 16)
            sp.sem_inc(x_out[1], 16)
            with sp.Fori(0, NIT) as it:
                sp.wait_ge(x_out[1], it * 16 + 16)
                sp.dma_start(xs[:, 1, :, :], x_d[it * 2 + 1]).then_inc(x_in[1], 16)
                sp.wait_ge(x_ffn, it * (JOBS * TT) + 4 * TT)
                sp.dma_start(out_d[it * 2], xs[:, 0, :, :]).then_inc(x_out[0], 16)
                sp.wait_ge(x_out[0], it * 16 + 16)
                sp.dma_start(xs[:, 0, :, :], x_d[((it + 1) % NIT) * 2]).then_inc(x_in[0], 16)
                sp.wait_ge(x_ffn, it * (JOBS * TT) + 5 * TT)
                sp.dma_start(out_d[it * 2 + 1], xs[:, 1, :, :]).then_inc(x_out[1], 16)
            sp.wait_ge(x_out[0], 16 * NIT)
            sp.wait_ge(x_out[1], 16 * NIT + 16)

        @block.gpsimd
        def _(pool):
            pool.iota(rowi[:, :], [[0, P]], base=0, channel_multiplier=1).then_inc(iotas, 1)
            pool.iota(coli[:, :], [[1, P]], base=0, channel_multiplier=0).then_inc(iotas, 1)
            pool.memset(mhalf[:, :], -0.5).then_inc(consts, 1)
            pool.memset(mone[:, :], -1.0).then_inc(consts, 1)
            pool.memset(eps[:, :], EPS).then_inc(consts, 1)

            def ln_scalars(L):
                pool.wait_ge(mv_ready, L * TT + TT)
                pool.tensor_tensor(ve[:, :], mv[:, :, 1], eps[:, :], ALU.add).then_inc(ln_small, 1)
                pool.tensor_tensor(nmean[:, :], mv[:, :, 0], mone[:, :], ALU.mult).then_inc(ln_small, 1)
                pool.wait_ge(ln_small, L * 4 + 2)
                pool.tensor_tensor(rstd[:, :], ve[:, :], mhalf[:, :], ALU.pow).then_inc(ln_small, 1)
                pool.wait_ge(ln_small, L * 4 + 3)
                pool.tensor_tensor(nmr[:, :], nmean[:, :], rstd[:, :], ALU.mult).then_inc(ln_small, 1)

            def scale_rows(q):
                half, kind = divmod(q, 2)
                pool.wait_ge(rinv_ready, q + 1)
                at = NC * kind + 4 * half
                w = wn[:, kind, 4 * half:4 * half + 4, :]
                pool.tensor_tensor(w, w, rinv[:, at:at + 4].unsqueeze(2).to_broadcast([P, 4, D]),
                                   ALU.mult).then_inc(w_scaled, 1)

            pool.wait_ge(consts, 3)
            scale_rows(0)
            scale_rows(1)
            ln_scalars(0)
            scale_rows(2)
            scale_rows(3)

            for s in range(3):
                h = 1 << s
                pool.wait_ge(wd_scaled, 2)
                if s:
                    pool.wait_ge(wd_bfl, 4 * s)
                if s == 1:
                    pool.wait_ge(mx_ready, 1)
                for b in range(2):
                    src = wds[:, (s + 1) % 2, b].rearrange("p (g a h) k -> p g a (h k)", a=2, h=h)
                    dst = wds[:, s % 2, b].rearrange("p (g a h) k -> p g a (h k)", a=2, h=h)
                    for a, op in enumerate((ALU.add, ALU.subtract)):
                        pool.tensor_tensor(dst[:, :, a], src[:, :, 0], src[:, :, 1], op).then_inc(wd_bfl, 1)

            pool.wait_ge(mx_ready, 2)
            pool.partition_all_reduce(mxg[:, :], mx[:, :], P, ABSMAX).then_inc(mxg_ready, 1)

            pool.wait_ge(mixk_ready, 1)
            pool.tensor_scalar(mxa[:, 0:D], rp[:, 0, :], w0s[:, 0:1], None, ALU.mult).then_inc(mix_chain, 1)
            pool.tensor_scalar(mxa[:, D:D + P], rp[:, 0, 0:P], w0s[:, 1:2], None, ALU.mult).then_inc(mix_chain, 1)
            pool.tensor_tensor(mxb[:, 0:D], rp[:, 1, :], mix_bc[:, 1, :], ALU.mult).then_inc(mix_chain, 1)
            pool.tensor_tensor(mxb[:, D:D + P], rp[:, 1, 0:P], mix_bc[:, 1, P:D], ALU.mult).then_inc(mix_chain, 1)
            pool.wait_ge(mix_chain, 4)
            pool.tensor_scalar(mxc[:, :], mxb[:, :], rpi[:, 1:2], None, ALU.mult).then_inc(mix_chain, 1)
            pool.wait_ge(mix_chain, 5)
            pool.tensor_tensor(mxb[:, :], mxa[:, :], mxc[:, :], ALU.add).then_inc(mix_chain, 1)
            pool.wait_ge(mix_chain, 6)
            pool.affine_select(out=mxa[:, 0:D], in_=mxb[:, 0:D], compare_op=ALU.is_ge, fill=0.0, base=0,
                               pattern=[[1, D]], channel_multiplier=-1).then_inc(mix_chain, 1)
            pool.affine_select(out=mxa[:, D:D + P], in_=mxb[:, D:D + P], compare_op=ALU.is_ge, fill=0.0, base=0,
                               pattern=[[1, P]], channel_multiplier=-1).then_inc(mix_chain, 1)
            pool.wait_ge(mix_chain, 8)
            pool.tensor_copy(wmix[:, HI, :], mxa[:, :]).then_inc(mix_chain, 1)
            pool.wait_ge(mix_chain, 9)
            pool.tensor_tensor(wmix[:, LO, :], mxa[:, :], wmix[:, HI, :], ALU.subtract).then_inc(wmix_ready, 1)

            with pool.Fori(0, NIT) as it:
                for jj, (fs, mid) in enumerate(PLAN):
                    ms = 1 - fs
                    L = it * LNS + LN_FIRST[jj]
                    ln_scalars(L)
                    if mid == "mix":
                        pool.wait_ge(xn_ready, L * TT + TT)
                        pool.tensor_tensor(xs[:, ms, :, :], xs[:, ms, :, :],
                                           bias[:, :].unsqueeze(1).to_broadcast([P, TT, D]),
                                           ALU.add).then_inc(bias_added, 1)
                        ln_scalars(L + 1)

        @block.tensor
        def _(pe):
            def transposes(L):
                pe.wait_ge(xn_ready, L * TT + TT)
                for kb in range(KB):
                    for t in range(TT):
                        last = pe.transpose(T[kb][:, t * P:(t + 1) * P], xn[:, t, kb * P:(kb + 1) * P], ident[:, :])
                    last.then_inc(tr_done, 1)

            pe.wait_ge(rows_in, 5 * 16)
            pe.wait_ge(ident_ready, 1)
            pe.transpose(T[0][:, 0:NROWS], rows[:, :], ident[0:NROWS, 0:NROWS]).then_inc(rows_T, 1)

            def w_transposes(q):
                half, kind = divmod(q, 2)
                pe.wait_ge(w_scaled, q + 1)
                if q == 0:
                    pe.wait_ge(cols_ready, 1)
                if q >= 2:
                    pe.wait_ge(bfl_ready, 2 * (q - 1))
                for kb in range(KB):
                    for i in range(4):
                        last = pe.transpose(TP[q % 2][kb][:, i * P:(i + 1) * P],
                                            wn[:, kind, 4 * half + i, kb * P:(kb + 1) * P], ident[:, :])
                last.then_inc(w_T, 1)

            def w_folds(q):
                pe.wait_ge(bfl_ready, 2 * (q + 1))
                if q == 0:
                    pe.wait_ge(had_ready, 1)
                if q >= 2:
                    pe.wait_ge(wlo_ready, 2 * (q - 1))
                for kb in range(KB):
                    last = pe.matmul(HP[q % 2][kb][:, :], had[:, :], bfl[:, q % 2, kb, :], start=True, stop=True)
                last.then_inc(w_fold, 1)

            w_transposes(0)
            w_transposes(1)
            w_folds(0)
            w_folds(1)
            w_transposes(2)
            w_folds(2)
            w_transposes(3)
            w_folds(3)
            pe.wait_ge(bfl_ready, 2 * NG)
            transposes(0)

            def wd_transposes(r):
                if r == 0:
                    pe.wait_ge(wd_bfl, 12)
                if r >= 2:
                    pe.wait_ge(wdT_ready, r - 1)
                for c in range(2):
                    for b in range(2):
                        last = pe.transpose(Dn[r % 2][:, (2 * c + b) * P:(2 * c + b + 1) * P],
                                            wds[:, 0, b, 2 * r + c, :], ident[:, :])
                last.then_inc(wd_T, 1)

            def wd_folds(r):
                pe.wait_ge(wdT_ready, r + 1)
                if r == 0:
                    pe.wait_ge(wlo_ready, 2 * (NG - 1))
                if r >= 2:
                    pe.wait_ge(wdlo_ready, 2 * (r - 1))
                pe.matmul(G[r % 2][:, :], had[:, :], wdT[:, r % 2, :], start=True, stop=True).then_inc(wd_fold, 1)

            for r in range(4):
                wd_transposes(r)
                if r:
                    wd_folds(r - 1)
            wd_folds(3)

            pe.wait_ge(wlo_ready, 2 * NG)
            pe.wait_ge(wdlo_ready, NC)

            def up_gate(K, c, fs):
                for kind, banks, freed, done in ((GATE, G, silu_ready, gate_done), (UP, U, a32_ready, up_done)):
                    if c >= 2:
                        pe.wait_ge(freed, K - 1)
                    n = 0
                    for kb in range(KB):
                        for w, h in ((HI, HI), (HI, LO), (LO, HI)):
                            mm = pe.matmul(banks[c % 2][:, :], wug[:, kind, w, kb, c * P:(c + 1) * P],
                                           xT[:, fs, h, kb, :], start=(n == 0), stop=(n == 5))
                            n += 1
                    mm.then_inc(done, 1)

            def down(K, c, J):
                pe.wait_ge(alo_ready, K + 1)
                if c == 0:
                    pe.wait_ge(x_ffn, J * TT + TT)
                for t in range(TT):
                    for n, (a, w) in enumerate(((HI, HI), (HI, LO), (LO, HI))):
                        mm = pe.matmul(Dn[t // 2][:, (t % 2) * D:(t % 2 + 1) * D], act[:, c, a, t * P:(t + 1) * P],
                                       wdn[:, c, w, :], start=(c == 0 and t % 2 == 0 and n == 0),
                                       stop=(c == NC - 1 and n == 2), skip_group_check=True)
                if c == NC - 1:
                    mm.then_inc(down_done, 1)

            def mix(ms):
                for t in range(TT):
                    n = 0
                    for kb in range(KB):
                        dst = T[t // 2][:, (t % 2) * D + kb * P:(t % 2 + 1) * D]
                        wc = slice(0, D) if kb == 0 else slice(D, D + P)
                        for a, w in ((HI, HI), (HI, LO), (LO, HI)):
                            mm = pe.matmul(dst, xT[:, ms, a, kb, t * P:(t + 1) * P], wmix[:, w, wc],
                                           start=(t % 2 == 0 and n == 0), stop=(n == 5), skip_group_check=True)
                            n += 1
                    if t % 2:
                        mm.then_inc(mix_done, 1)

            with pe.Fori(0, NIT) as it:
                for jj, (fs, mid) in enumerate(PLAN):
                    ms = 1 - fs
                    J = it * JOBS + jj
                    L = it * LNS + LN_FIRST[jj]
                    LM = L + (mid == "mix")
                    pe.wait_ge(xTlo_ready, L * KB)
                    for c in range(NC):
                        K = it * (JOBS * NC) + jj * NC + c
                        up_gate(K, c, fs)
                        if mid == "mix" and c == 2:
                            transposes(L)
                        if mid == "mix" and c == 3:
                            pe.wait_ge(xTlo_ready, L * KB + KB)
                            if jj == 1:
                                pe.wait_ge(wmix_ready, 1)
                            mix(ms)
                        if c == 6:
                            transposes(LM)
                        if c >= LAG:
                            down(K - LAG, c - LAG, J)
                    for c in range(NC - LAG, NC):
                        down(it * (JOBS * NC) + jj * NC + c, c, J)

        @block.scalar
        def _(sc):
            sc.dma_start(su_bc[:, :], su_ug.rearrange("(a d) -> a d", a=1).to_broadcast([P, D])).then_inc(bc_in, 16)
            sc.dma_start(mix_bc[:, :, :].rearrange("p a d -> p (a d)"),
                         mix_w.rearrange("(o a) d -> o (a d)", o=1).to_broadcast([P, 2 * D])).then_inc(bc_in, 16)
            sc.dma_start(dec_bc[:, :], decay.rearrange("a o -> o a").to_broadcast([P, 2])).then_inc(bc_in, 16)
            sc.dma_start(bias[:, :], mix_b.rearrange("(a d) -> a d", a=1).to_broadcast([P, D])).then_inc(bc_in, 16)

            def normalise(L, slot):
                sc.wait_ge(ln_small, L * 4 + 4)
                for t in range(TT):
                    sc.activation(xn[:, t, :], xs[:, slot, t, :], ACT.Identity, bias=nmr[:, t:t + 1],
                                  scale=rstd[:, t:t + 1]).then_inc(xn_ready, 1)

            def xT_hi(L, slot):
                for kb in range(KB):
                    sc.wait_ge(tr_done, L * KB + kb + 1)
                    sc.activation(xT[:, slot, HI, kb, :], T[kb][:, :], ACT.Copy, scale=XS).then_inc(xThi_ready, 1)

            def wTa_copy(q):
                sc.wait_ge(w_T, q + 1)
                if q >= 2:
                    sc.wait_ge(bfl_ready, 2 * (q - 1))
                sc.copy(wTa[:, q % 2, :], TP[q % 2][0][:, :]).then_inc(wTa_ready, 1)

            def w_hi(q):
                half, kind = divmod(q, 2)
                sc.wait_ge(w_fold, q + 1)
                sc.wait_ge(sk_ready, 1)
                for kb in range(KB):
                    sc.activation(wug[:, kind, HI, kb, 512 * half:512 * half + 512], HP[q % 2][kb][:, :], ACT.Copy,
                                  scale=sk[:, kb:kb + 1]).then_inc(whi_ready, 1)

            for q in range(NG):
                wTa_copy(q)
                if q == 2:
                    normalise(0, 0)
                if q:
                    w_hi(q - 1)
            w_hi(NG - 1)
            xT_hi(0, 0)

            def wdT_copy(r):
                sc.wait_ge(wd_T, r + 1)
                if r >= 2:
                    sc.wait_ge(wd_fold, r - 1)
                sc.copy(wdT[:, r % 2, :], Dn[r % 2][:, :]).then_inc(wdT_ready, 1)

            def wd_hi(r):
                sc.wait_ge(wd_fold, r + 1)
                if r == 0:
                    sc.wait_ge(feta_ready, 1)
                for c in range(2):
                    sc.activation(wdn[:, 2 * r + c, HI, :], G[r % 2][:, c * D:(c + 1) * D], ACT.Copy,
                                  scale=feta[:, 2 * r + c:2 * r + c + 1]).then_inc(wdhi_ready, 1)

            for r in range(4):
                wdT_copy(r)
                if r:
                    wd_hi(r - 1)
            wd_hi(3)
            sc.wait_ge(scales_ready, 1)

            with sc.Fori(0, NIT) as it:
                for jj, (fs, mid) in enumerate(PLAN):
                    ms = 1 - fs
                    L = it * LNS + LN_FIRST[jj]
                    LM = L + (mid == "mix")
                    for c in range(NC):
                        K = it * (JOBS * NC) + jj * NC + c
                        if mid == "mix" and c == 3:
                            xT_hi(L, ms)
                        if c == 7:
                            xT_hi(LM, ms)
                        sc.wait_ge(gate_done, K + 1)
                        if c >= 2:
                            sc.wait_ge(a32_ready, K - 1)
                        sc.activation(sil[:, c % 2, :], G[c % 2][:, :], ACT.Silu,
                                      scale=sug[:, NC + c:NC + c + 1]).then_inc(silu_ready, 1)
                        if mid == "mix" and c == 1:
                            normalise(L, ms)
                        if c == 5:
                            normalise(LM, ms)
                        sc.wait_ge(a32_ready, K + 1)
                        sc.copy(act[:, c, HI, :], a32[:, c % 2, :]).then_inc(ahi_ready, 1)

        @block.vector
        def _(dve):
            count = [0]

            def chained(ins):
                count[0] += 1
                ins.then_inc(dve_chain, 1)
                dve.wait_ge(dve_chain, count[0])

            dve.wait_ge(iotas, 2)
            dve.tensor_tensor(ident[:, :], rowi[:, :], coli[:, :], ALU.is_equal).then_inc(ident_ready, 1)
            chained(dve.tensor_tensor(par[:, :], rowi[:, :], coli[:, :], ALU.bitwise_and))
            for s in (4, 2, 1):
                chained(dve.tensor_scalar(part[:, :], par[:, :], s, None, ALU.logical_shift_right))
                chained(dve.tensor_tensor(par[:, :], par[:, :], part[:, :], ALU.bitwise_xor))
            chained(dve.tensor_scalar(part[:, :], par[:, :], 1, None, ALU.bitwise_and))
            dve.tensor_scalar(had[:, :], part[:, :], -2.0, 1.0, ALU.mult, ALU.add).then_inc(had_ready, 1)

            def row_max(q):
                half, kind = divmod(q, 2)
                at = NC * kind + 4 * half
                dve.wait_ge(wn_in[q], 16)
                chained(dve.tensor_reduce(rmax[:, at:at + 4], wn[:, kind, 4 * half:4 * half + 4, :], AX_X, ALU.max,
                                          apply_absolute_value=True))
                chained(dve.tensor_scalar(rmax[:, at:at + 4], rmax[:, at:at + 4], TINY, None, ALU.max))
                dve.reciprocal(rinv[:, at:at + 4], rmax[:, at:at + 4]).then_inc(rinv_ready, 1)

            def butterfly(q):
                dve.wait_ge(wTa_ready, q + 1)
                if q >= 2:
                    dve.wait_ge(w_fold, q - 1)
                for kb, op in ((0, ALU.add), (1, ALU.subtract)):
                    dve.tensor_tensor(bfl[:, q % 2, kb, :], wTa[:, q % 2, :], TP[q % 2][1][:, :], op)\
                       .then_inc(bfl_ready, 1)

            def w_lo(q):
                half, kind = divmod(q, 2)
                for kb in range(KB):
                    at = slice(512 * half, 512 * half + 512)
                    dve.wait_ge(whi_ready, KB * q + kb + 1)
                    dve.scalar_tensor_tensor(wug[:, kind, LO, kb, at], HP[q % 2][kb][:, :], sk[:, kb:kb + 1],
                                             wug[:, kind, HI, kb, at], ALU.mult, ALU.subtract).then_inc(wlo_ready, 1)

            def layer_stats(slot):
                for t in range(TT):
                    dve.bn_stats(stats[:, t, :], xs[:, slot, t, :]).then_inc(stats_ready, 1)

            def mean_var():
                for t in range(TT):
                    dve.bn_aggr(mv[:, t, :], stats[:, t, :]).then_inc(mv_ready, 1)

            def xT_lo(L, slot):
                for kb in range(KB):
                    dve.wait_ge(xThi_ready, L * KB + kb + 1)
                    dve.scalar_tensor_tensor(xT[:, slot, LO, kb, :], T[kb][:, :], XS, xT[:, slot, HI, kb, :],
                                             ALU.mult, ALU.subtract).then_inc(xTlo_ready, 1)

            row_max(0)
            row_max(1)
            dve.wait_ge(bc_in, 4 * 16)
            chained(dve.tensor_reduce(sumx[:, :], su_bc[:, :], AX_X, ALU.max, apply_absolute_value=True))
            chained(dve.tensor_scalar(sumx[:, :], sumx[:, :], TINY, None, ALU.max))
            chained(dve.reciprocal(suinv[:, :], sumx[:, :]))
            dve.wait_ge(rows_T, 1)
            dve.tensor_copy(cols[:, :], T[0][:, 0:NROWS]).then_inc(cols_ready, 1)
            dve.wait_ge(cols_ready, 1)
            dve.tensor_scalar(sk[:, :], cols[:, C_SUG], suinv[:, 0:1], WS, ALU.mult, ALU.mult).then_inc(sk_ready, 1)
            dve.wait_ge(sk_ready, 1)
            row_max(2)
            butterfly(0)
            dve.wait_ge(x_in[0], 16)
            layer_stats(0)
            dve.wait_ge(stats_ready, TT)
            mean_var()
            row_max(3)
            butterfly(1)
            w_lo(0)
            butterfly(2)
            w_lo(1)

            dve.wait_ge(wd_in, 16)
            for b in range(2):
                dve.tensor_scalar(wds[:, 1, b], wds[:, 0, b], cols[:, C_WSD.start + b:C_WSD.start + b + 1], None,
                                  ALU.mult).then_inc(wd_scaled, 1)
            butterfly(3)
            w_lo(2)
            dve.wait_ge(wd_scaled, 2)
            dve.tensor_reduce(mx[:, 1:2], wds[:, 1].rearrange("p b c k -> p (b c k)"), AX_X, ALU.max,
                              apply_absolute_value=True).then_inc(mx_ready, 1)
            w_lo(3)

            chained(dve.tensor_tensor(sug[:, :], rmax[:, :], cols[:, C_WS], ALU.mult))
            chained(dve.tensor_scalar(sug[:, :], sug[:, :], sumx[:, 0:1], 1.0 / (16.0 * XS * WS), ALU.mult, ALU.mult))
            PS_TOP = 256.0 * 16.0 * XS * WS
            chained(dve.scalar_tensor_tensor(asg[:, :], sug[:, NC:2 * NC], -1.0, sug[:, NC:2 * NC],
                                             ALU.mult, ALU.max))
            chained(dve.tensor_scalar(asg[:, :], asg[:, :], TINY, None, ALU.max))
            chained(dve.reciprocal(asgi[:, :], asg[:, :]))
            chained(dve.tensor_scalar(beta[:, :], asgi[:, :], F16_TOP / PS_TOP / PS_TOP, None, ALU.mult))
            chained(dve.scalar_tensor_tensor(fch[:, :], sug[:, 0:NC], PS_TOP * PS_TOP / F16_TOP, asg[:, :],
                                             ALU.mult, ALU.mult))
            chained(dve.tensor_tensor(fch[:, :], fch[:, :], cols[:, C_SUD], ALU.mult))
            dve.tensor_reduce(mx[:, 0:1], fch[:, :], AX_X, ALU.max, apply_absolute_value=True).then_inc(mx_ready, 1)

            xT_lo(0, 0)

            chained(dve.tensor_scalar(pw[:, 0, :], dec_bc[:, :], 0.9, 1.0, ALU.max, ALU.min))
            chained(dve.memset(rp[:, :, 0:1], 1.0))
            for k in range(8):
                n = 1 << k
                for d in range(2):
                    chained(dve.tensor_scalar(rp[:, d, n:2 * n], rp[:, d, 0:n], pw[:, k, d:d + 1], None, ALU.mult))
                chained(dve.tensor_tensor(pw[:, k + 1, :], pw[:, k, :], pw[:, k, :], ALU.mult))
            for d in range(2):
                chained(dve.tensor_tensor(dg[:, d, :], rp[:, d, 0:P], ident[:, :], ALU.mult))
            chained(dve.tensor_reduce(rpd[:, :], dg[:, :, :], AX_X, ALU.add))
            chained(dve.reciprocal(rpi[:, :], rpd[:, :]))
            chained(dve.tensor_reduce(mmx[:, :], mix_bc[:, :, :], AX_X, ALU.max, apply_absolute_value=True))
            chained(dve.tensor_scalar(msum[:, :], mmx[:, 0:1], mmx[:, 1:2], TINY, ALU.add, ALU.max))
            chained(dve.reciprocal(minv[:, :], msum[:, :]))
            chained(dve.tensor_scalar(kmix[:, :], msum[:, :], 1.0 / (MIX_TOP * XS), None, ALU.mult))
            chained(dve.tensor_scalar(rpi[:, :], rpi[:, :], minv[:, 0:1], MIX_TOP, ALU.mult, ALU.mult))
            dve.tensor_scalar(w0s[:, :], cols[:, C_W0], rpi[:, 0:1], None, ALU.mult).then_inc(mixk_ready, 1)

            dve.wait_ge(mxg_ready, 1)
            chained(dve.tensor_scalar(fall[:, :], mxg[:, 0:1], mxg[:, 1:2], TINY, ALU.mult, ALU.max))
            chained(dve.reciprocal(finv[:, :], fall[:, :]))
            dve.tensor_scalar(feta[:, :], fch[:, :], finv[:, 0:1], F16_TOP / INTER, ALU.mult, ALU.mult)\
               .then_inc(feta_ready, 1)
            dve.tensor_scalar(kdown[:, :], fall[:, :], 0.5 / 32.0 * INTER / F16_TOP, None, ALU.mult)\
               .then_inc(scales_ready, 1)
            dve.wait_ge(feta_ready, 1)
            dve.wait_ge(scales_ready, 1)
            for c in range(NC):
                dve.wait_ge(wdhi_ready, 2 * (c // 2) + 2)
                dve.scalar_tensor_tensor(wdn[:, c, LO, :], G[(c // 2) % 2][:, (c % 2) * D:(c % 2 + 1) * D],
                                         feta[:, c:c + 1], wdn[:, c, HI, :], ALU.mult, ALU.subtract)\
                   .then_inc(wdlo_ready, 1)

            dve.sem_inc(x_ffn, TT)
            with dve.Fori(0, NIT) as it:
                for jj, (fs, mid) in enumerate(PLAN):
                    ms = 1 - fs
                    J = it * JOBS + jj
                    L = it * LNS + LN_FIRST[jj]
                    LM = L + (mid == "mix")
                    M = it * MIXS + (jj == 2)
                    for c in range(NC):
                        K = it * (JOBS * NC) + jj * NC + c
                        if mid == "mix" and c == 3:
                            xT_lo(L, ms)
                        if mid == "mix" and c == 4:
                            dve.wait_ge(bias_added, M + 1)
                            for t in range(TT):
                                dve.wait_ge(mix_done, M * 2 + t // 2 + 1)
                                dve.scalar_tensor_tensor(xs[:, ms, t, :], T[t // 2][:, (t % 2) * D:(t % 2 + 1) * D],
                                                         kmix[:, 0:1], xs[:, ms, t, :], ALU.mult, ALU.add)\
                                   .then_inc(x_mix, 1)
                        if c == 7:
                            xT_lo(LM, ms)
                        dve.wait_ge(up_done, K + 1)
                        dve.wait_ge(silu_ready, K + 1)
                        dve.scalar_tensor_tensor(a32[:, c % 2, :], U[c % 2][:, :], beta[:, c:c + 1], sil[:, c % 2, :],
                                                 ALU.mult, ALU.mult).then_inc(a32_ready, 1)
                        if mid == "mix" and c == 0:
                            dve.wait_ge(x_ffn, J * TT + TT)
                            layer_stats(ms)
                        if c == 4:
                            if mid == "mix":
                                dve.wait_ge(x_mix, M * TT + TT)
                            elif ms == 0:
                                dve.wait_ge(x_in[0], it * 16 + 32)
                            else:
                                dve.wait_ge(x_in[1], it * 16 + 16)
                            layer_stats(ms)
                        ln = L if mid == "mix" and c == 0 else LM if c == 4 else None
                        if ln is not None:
                            dve.wait_ge(stats_ready, ln * TT + TT)
                        dve.wait_ge(ahi_ready, K + 1)
                        dve.tensor_tensor(act[:, c, LO, :], a32[:, c % 2, :], act[:, c, HI, :], ALU.subtract)\
                           .then_inc(alo_ready, 1)
                        if ln is not None:
                            mean_var()
                    dve.wait_ge(down_done, J + 1)
                    for t in range(TT):
                        dve.scalar_tensor_tensor(xs[:, fs, t, :], Dn[t // 2][:, (t % 2) * D:(t % 2 + 1) * D],
                                                 kdown[:, 0:1], xs[:, fs, t, :], ALU.mult, ALU.add).then_inc(x_ffn, 1)


_INS = ['L0_attn_x', 'L0_attn_weight', 'L0_attn_bias', 'L0_attn_decay_value', 'L0_ffn_SU_ug', 'L0_ffn_SU_dp',
        'L0_ffn_Wscale_ug', 'L0_ffn_Wscale_dp', 'L0_ffn_W_up', 'L0_ffn_W_gate', 'L0_ffn_W_down']
_OUTS = [((16, 256, 256), 'float32')]


def kernel(**inputs):
    import numpy as _np
    import concourse.bacc as _bacc
    from concourse import mybir as _mybir
    from concourse.bass_utils import run_bass_kernel_spmd as _run

    nc = _bacc.Bacc("TRN2", target_bir_lowering=False, num_devices=1)
    arrays, args = {}, []
    for name in _INS:
        a = _np.ascontiguousarray(inputs[name])
        arrays[f"in_{name}_dram"] = a
        args.append(nc.dram_tensor(f"in_{name}_dram", a.shape, _mybir.dt.from_np(a.dtype), kind="ExternalInput").ap())
    for i, (shape, dtype) in enumerate(_OUTS):
        dt = _mybir.dt.from_np(_np.dtype(dtype))
        args.append(nc.dram_tensor(f"out_{i}_dram", shape, dt, kind="ExternalOutput").ap())
    macaron_kernel(nc, *args)
    r = _run(nc, [arrays], core_ids=[0])
    got = tuple(r.results[0][f"out_{i}_dram"] for i in range(len(_OUTS)))
    return got[0]
```

```python
from contextlib import ExitStack

import concourse.bass as bass
from concourse import mybir

ALU = mybir.AluOpType
ACT = mybir.ActivationFunctionType
F32 = mybir.dt.float32
F16 = mybir.dt.float16
I32 = mybir.dt.int32
AX_X = mybir.AxisListType.X
ABSMAX = bass.bass_isa.ReduceOp.absmax

P = 128
EPS = 1e-5
TINY = 1e-30
NORM_MIN = 1e-18

XS = 2.0 ** 10
WS = 2.0 ** 7
F16_TOP = 2.0 ** 15
MIX_TOP = 2.0 ** 14

HI, LO = 0, 1
UP, GATE = 0, 1


def macaron_kernel(nc, x, mix_w, mix_b, decay, su_ug, su_dp, ws_ug, ws_dp, w_up, w_gate, w_down, out):
    B, E, D = x.shape
    INTER = w_up.shape[0]
    TT = 4
    SLOT = TT * P
    NIT = B * E // (2 * SLOT)
    KB = D // P
    NC = INTER // P
    NG = 4
    JOBS = 4
    LNS = 6
    MIXS = 2
    WD_TOP = (INTER // 2) ** 0.5
    LAG = 2

    PLAN = [(0, "load"), (1, "mix"), (0, "mix"), (1, "load")]
    LN_FIRST = [1, 2, 4, 6]

    x_d = x.rearrange("b e d -> (b e) d").rearrange("(g p t) d -> g p t d", p=P, t=TT)
    out_d = out.rearrange("b e d -> (b e) d").rearrange("(g p t) d -> g p t d", p=P, t=TT)
    w_d = {UP: w_up.rearrange("(m p) d -> p m d", p=P), GATE: w_gate.rearrange("(m p) d -> p m d", p=P)}
    wd_d = w_down.rearrange("(b p) n -> p b n", p=P)

    ctx = ExitStack()
    with ctx:
        def sb(name, shape, dt=F32):
            return ctx.enter_context(nc.sbuf_tensor(name, shape, dt))

        def sem(name):
            return ctx.enter_context(nc.semaphore(name))

        xs = sb("xs", [P, 2, TT, D])
        xn = sb("xn", [P, TT, D])
        xh = sb("xh", [P, TT, D], F16)
        xl = sb("xl", [P, TT, D], F16)
        xT = sb("xT", [P, 2, 2, KB, SLOT], F16)
        act = sb("act", [P, NC, 2, SLOT], F16)
        sil = sb("sil", [P, 2, SLOT])
        a32 = sb("a32", [P, 2, SLOT])
        wug = sb("wug", [P, 2, 2, KB, INTER], F16)
        wdn = sb("wdn", [P, NC, 2, D], F16)
        wmix = sb("wmix", [P, 2, D + P], F16)
        bias = sb("bias", [P, D])
        stats = sb("stats", [P, TT, 6])
        mv = sb("mv", [P, TT, 2])
        ve = sb("ve", [P, TT])
        nmean = sb("nmean", [P, TT])
        rstd = sb("rstd", [P, TT])
        nmr = sb("nmr", [P, TT])
        mhalf = sb("mhalf", [P, TT])
        half = sb("half", [P, 1])
        warm = sb("warm", [P, 1])
        mone = sb("mone", [P, TT])
        wn = sb("wn", [P, 2, NC, D])
        wds = sb("wds", [P, 2, 2, NC, P])
        wTa = sb("wTa", [P, 2, SLOT])
        bfl = sb("bfl", [P, 2, 2, SLOT])
        wdT = sb("wdT", [P, 2, SLOT])
        rowi = sb("rowi", [P, P], I32)
        coli = sb("coli", [P, P], I32)
        par = sb("par", [P, P], I32)
        part = sb("part", [P, P], I32)
        had = sb("had", [P, P])
        ident = sb("ident", [P, P])
        ident16 = sb("ident16", [P, P], F16)
        NROWS = 2 * NC + KB + NC + KB + KB
        rows = sb("rows", [NROWS, P])
        cols = sb("cols", [P, NROWS])
        su_bc = sb("su_bc", [P, D])
        mix_bc = sb("mix_bc", [P, 2, D])
        dec_bc = sb("dec_bc", [P, 2])
        rmax = sb("rmax", [P, 2 * NC])
        rinv = sb("rinv", [P, 2 * NC])
        sumx = sb("sumx", [P, 1])
        suinv = sb("suinv", [P, 1])
        sk = sb("sk", [P, KB])
        sug = sb("sug", [P, 2 * NC])
        asg = sb("asg", [P, NC])
        asgi = sb("asgi", [P, NC])
        beta = sb("beta", [P, NC])
        fch = sb("fch", [P, NC])
        feta = sb("feta", [P, NC])
        mx = sb("mx", [P, 2])
        mxg = sb("mxg", [P, 2])
        wdss = sb("wdss", [P, 2])
        wdnorm = sb("wdnorm", [P, 1])
        fall = sb("fall", [P, 1])
        finv = sb("finv", [P, 1])
        kdown = sb("kdown", [P, 1])
        pw = sb("pw", [P, 9, 2])
        rp = sb("rp", [P, 2, D])
        dg = sb("dg", [P, 2, P])
        rpd = sb("rpd", [P, 2])
        rpi = sb("rpi", [P, 2])
        mmx = sb("mmx", [P, 2])
        msum = sb("msum", [P, 1])
        minv = sb("minv", [P, 1])
        kmix = sb("kmix", [P, 1])
        w0s = sb("w0s", [P, KB])
        mxa = sb("mxa", [P, D + P])
        mxb = sb("mxb", [P, D + P])
        mxc = sb("mxc", [P, D + P])

        C_WS = slice(0, 2 * NC)
        C_SUG = slice(2 * NC, 2 * NC + KB)
        C_SUD = slice(2 * NC + KB, 3 * NC + KB)
        C_WSD = slice(3 * NC + KB, 3 * NC + 2 * KB)
        C_W0 = slice(3 * NC + 2 * KB, 3 * NC + 3 * KB)

        G = [ctx.enter_context(nc.psum_tensor(f"G{i}", [P, 512], F32)) for i in range(2)]
        U = [ctx.enter_context(nc.psum_tensor(f"U{i}", [P, 512], F32)) for i in range(2)]
        Dn = [ctx.enter_context(nc.psum_tensor(f"Dn{i}", [P, 512], F32)) for i in range(2)]
        T = [ctx.enter_context(nc.psum_tensor(f"T{i}", [P, 512], F32)) for i in range(2)]
        TH = [t[:, :].bitcast(F16).rearrange("p (h s) -> p h s", h=2) for t in T]
        TP = [T, Dn]
        HP = [G, U]
        TWD = [Dn[0], Dn[1], G[0], G[1]]
        HWD = [T[0], T[1], Dn[0], Dn[1]]

        wn_in = [sem(f"wn_in{q}") for q in range(NG)]
        wd_in = [sem(f"wd_in{b}") for b in range(2)]
        rows_in = sem("rows_in")
        dec_in = sem("dec_in")
        su_in = sem("su_in")
        mix_in = sem("mix_in")
        x_in = [sem("x_in0"), sem("x_in1")]
        x_out = [sem("x_out0"), sem("x_out1")]
        iotas = sem("iotas")
        consts = sem("consts")
        had_ready = sem("had_ready")
        ident_ready = sem("ident_ready")
        rows_T = sem("rows_T")
        cols_ready = sem("cols_ready")
        sk_ready = sem("sk_ready")
        rinv_ready = sem("rinv_ready")
        w_scaled = sem("w_scaled")
        w_T = sem("w_T")
        wTa_ready = sem("wTa_ready")
        bfl_ready = sem("bfl_ready")
        w_fold = sem("w_fold")
        whi_ready = sem("whi_ready")
        wlo_ready = sem("wlo_ready")
        mx_ready = sem("mx_ready")
        mxg_ready = sem("mxg_ready")
        wd_scaled = sem("wd_scaled")
        wd_sq = sem("wd_sq")
        wd_bfl = sem("wd_bfl")
        wd_T = sem("wd_T")
        wdT_ready = sem("wdT_ready")
        wd_fold = sem("wd_fold")
        feta_ready = sem("feta_ready")
        wdhi_ready = sem("wdhi_ready")
        wdlo_ready = sem("wdlo_ready")
        scales_ready = sem("scales_ready")
        pow_chain = sem("pow_chain")
        dg_ready = sem("dg_ready")
        mixk_ready = sem("mixk_ready")
        mix_chain = sem("mix_chain")
        wmix_ready = sem("wmix_ready")
        dve_chain = sem("dve_chain")

        gate_done = sem("gate_done")
        up_done = sem("up_done")
        down_done = sem("down_done")
        tr_done = sem("tr_done")
        mix_done = sem("mix_done")
        silu_ready = sem("silu_ready")
        ahi_ready = sem("ahi_ready")
        xn_ready = sem("xn_ready")
        xTa_ready = sem("xTa_ready")
        a32_ready = sem("a32_ready")
        alo_ready = sem("alo_ready")
        x_ffn = sem("x_ffn")
        x_mix = sem("x_mix")
        stats_ready = sem("stats_ready")
        mv_ready = sem("mv_ready")
        xhl_ready = sem("xhl_ready")
        xTb_ready = sem("xTb_ready")
        stats_seen = sem("stats_seen")
        ln_small = sem("ln_small")
        bias_added = sem("bias_added")

        block = ctx.enter_context(nc.Block())

        @block.sync
        def _(sp):
            def load_w(q):
                hf, kind = divmod(q, 2)
                sp.dma_start(wn[:, kind, 4 * hf:4 * hf + 4, :],
                             w_d[kind][:, 4 * hf:4 * hf + 4, :]).then_inc(wn_in[q], 16)

            def load_wd(b):
                sp.dma_start(wds[:, 0, b].rearrange("p c k -> p (c k)"), wd_d[:, b, :]).then_inc(wd_in[b], 16)

            load_w(0)
            sp.dma_start(rows[0:2 * NC, :], ws_ug.rearrange("(r c) -> r c", c=P)).then_inc(rows_in, 16)
            sp.dma_start(rows[C_SUG, :], su_ug.rearrange("(r c) -> r c", c=P)).then_inc(rows_in, 16)
            load_w(1)
            sp.dma_start(rows[C_SUD, :], su_dp.rearrange("(r c) -> r c", c=P)).then_inc(rows_in, 16)
            sp.dma_start(rows[C_WSD, :], ws_dp.rearrange("(r c) -> r c", c=P)).then_inc(rows_in, 16)
            sp.dma_start(rows[C_W0, :], mix_w[0:1, :].rearrange("a (r c) -> (a r) c", c=P)).then_inc(rows_in, 16)
            sp.dma_start(dec_bc[:, :], decay.rearrange("a o -> o a").to_broadcast([P, 2])).then_inc(dec_in, 16)
            load_wd(0)
            sp.dma_start(su_bc[:, :], su_ug.rearrange("(a d) -> a d", a=1).to_broadcast([P, D])).then_inc(su_in, 16)
            load_wd(1)
            load_w(2)
            load_w(3)
            sp.dma_start(xs[:, 0, :, :], x_d[0]).then_inc(x_in[0], 16)
            sp.dma_start(mix_bc[:, :, :].rearrange("p a d -> p (a d)"),
                         mix_w.rearrange("(o a) d -> o (a d)", o=1).to_broadcast([P, 2 * D])).then_inc(mix_in, 16)
            sp.dma_start(bias[:, :], mix_b.rearrange("(a d) -> a d", a=1).to_broadcast([P, D])).then_inc(mix_in, 16)
            sp.sem_inc(x_out[1], 16)
            with sp.Fori(0, NIT) as it:
                sp.wait_ge(x_out[1], it * 16 + 16)
                sp.dma_start(xs[:, 1, :, :], x_d[it * 2 + 1]).then_inc(x_in[1], 16)
                sp.wait_ge(x_ffn, it * (JOBS * TT) + 4 * TT)
                sp.dma_start(out_d[it * 2], xs[:, 0, :, :]).then_inc(x_out[0], 16)
                sp.wait_ge(x_out[0], it * 16 + 16)
                sp.dma_start(xs[:, 0, :, :], x_d[((it + 1) % NIT) * 2]).then_inc(x_in[0], 16)
                sp.wait_ge(x_ffn, it * (JOBS * TT) + 5 * TT)
                sp.dma_start(out_d[it * 2 + 1], xs[:, 1, :, :]).then_inc(x_out[1], 16)
            sp.wait_ge(x_out[0], 16 * NIT)
            sp.wait_ge(x_out[1], 16 * NIT + 16)

        @block.gpsimd
        def _(pool):
            pool.iota(rowi[:, :], [[0, P]], base=0, channel_multiplier=1).then_inc(iotas, 1)
            pool.iota(coli[:, :], [[1, P]], base=0, channel_multiplier=0).then_inc(iotas, 1)
            pool.memset(mhalf[:, :], -0.5).then_inc(consts, 1)
            pool.memset(mone[:, :], -1.0).then_inc(consts, 1)
            pool.memset(half[:, :], 0.5).then_inc(consts, 1)

            def ln_scalars(L):
                pool.wait_ge(mv_ready, L * TT + TT)
                pool.tensor_tensor(nmean[:, :], mv[:, :, 0], mone[:, :], ALU.mult).then_inc(ln_small, 1)
                pool.tensor_scalar(ve[:, :], mv[:, :, 1], EPS, 1.0 / (XS * XS), ALU.add, ALU.mult)\
                    .then_inc(ln_small, 1)
                pool.wait_ge(ln_small, L * 4 + 2)
                pool.tensor_tensor(rstd[:, :], ve[:, :], mhalf[:, :], ALU.pow).then_inc(ln_small, 1)
                pool.wait_ge(ln_small, L * 4 + 3)
                pool.tensor_tensor(nmr[:, :], nmean[:, :], rstd[:, :], ALU.mult).then_inc(ln_small, 1)

            pool.wait_ge(consts, 3)
            pool.wait_ge(dec_in, 16)
            pool.tensor_scalar(pw[:, 0, :], dec_bc[:, :], 0.9, 1.0, ALU.max, ALU.min).then_inc(pow_chain, 1)
            pool.memset(rp[:, :, 0:1], 1.0).then_inc(pow_chain, 1)
            for k in range(8):
                n = 1 << k
                pool.wait_ge(pow_chain, 2 * k + 2)
                pool.tensor_tensor(rp[:, :, n:2 * n], rp[:, :, 0:n],
                                   pw[:, k, :].unsqueeze(2).to_broadcast([P, 2, n]), ALU.mult).then_inc(pow_chain, 1)
                pool.tensor_tensor(pw[:, k + 1, :], pw[:, k, :], pw[:, k, :], ALU.mult).then_inc(pow_chain, 1)
            pool.wait_ge(pow_chain, 18)
            pool.wait_ge(ident_ready, 1)
            pool.tensor_tensor(dg[:, :, :], rp[:, :, 0:P], ident[:, :].unsqueeze(1).to_broadcast([P, 2, P]),
                               ALU.mult).then_inc(dg_ready, 1)

            for s in range(3):
                h = 1 << s
                if s == 2:
                    pool.wait_ge(wd_sq, 2)
                for b in range(2):
                    if s == 0:
                        pool.wait_ge(wd_scaled, b + 1)
                    else:
                        pool.wait_ge(wd_bfl, 4 * s - 2 + 2 * b)
                    src = wds[:, (s + 1) % 2, b].rearrange("p (g a h) k -> p g a (h k)", a=2, h=h)
                    dst = wds[:, s % 2, b].rearrange("p (g a h) k -> p g a (h k)", a=2, h=h)
                    for a, op in enumerate((ALU.add, ALU.subtract)):
                        pool.tensor_tensor(dst[:, :, a], src[:, :, 0], src[:, :, 1], op).then_inc(wd_bfl, 1)
                if s == 0:
                    ln_scalars(0)
            pool.wait_ge(mx_ready, 2)
            pool.partition_all_reduce(mxg[:, :], mx[:, :], P, ABSMAX).then_inc(mxg_ready, 1)
            pool.wait_ge(mxg_ready, 1)
            pool.tensor_tensor(wdnorm[:, :], mxg[:, 1:2], half[:, :], ALU.pow).then_inc(mxg_ready, 1)

            pool.wait_ge(mixk_ready, 1)
            pool.tensor_scalar(mxa[:, 0:D], rp[:, 0, :], w0s[:, 0:1], None, ALU.mult).then_inc(mix_chain, 1)
            pool.tensor_scalar(mxa[:, D:D + P], rp[:, 0, 0:P], w0s[:, 1:2], None, ALU.mult).then_inc(mix_chain, 1)
            pool.tensor_tensor(mxb[:, 0:D], rp[:, 1, :], mix_bc[:, 1, :], ALU.mult).then_inc(mix_chain, 1)
            pool.tensor_tensor(mxb[:, D:D + P], rp[:, 1, 0:P], mix_bc[:, 1, P:D], ALU.mult).then_inc(mix_chain, 1)
            pool.wait_ge(mix_chain, 4)
            pool.tensor_scalar(mxc[:, :], mxb[:, :], rpi[:, 1:2], None, ALU.mult).then_inc(mix_chain, 1)
            pool.wait_ge(mix_chain, 5)
            pool.tensor_tensor(mxb[:, :], mxa[:, :], mxc[:, :], ALU.add).then_inc(mix_chain, 1)
            pool.wait_ge(mix_chain, 6)
            pool.affine_select(out=mxa[:, 0:D], in_=mxb[:, 0:D], compare_op=ALU.is_ge, fill=0.0, base=0,
                               pattern=[[1, D]], channel_multiplier=-1).then_inc(mix_chain, 1)
            pool.affine_select(out=mxa[:, D:D + P], in_=mxb[:, D:D + P], compare_op=ALU.is_ge, fill=0.0, base=0,
                               pattern=[[1, P]], channel_multiplier=-1).then_inc(mix_chain, 1)
            pool.wait_ge(mix_chain, 8)
            pool.tensor_copy(wmix[:, HI, :], mxa[:, :]).then_inc(mix_chain, 1)
            pool.wait_ge(mix_chain, 9)
            pool.tensor_tensor(wmix[:, LO, :], mxa[:, :], wmix[:, HI, :], ALU.subtract).then_inc(wmix_ready, 1)

            with pool.Fori(0, NIT) as it:
                for jj, (fs, mid) in enumerate(PLAN):
                    ms = 1 - fs
                    L = it * LNS + LN_FIRST[jj]
                    ln_scalars(L)
                    if mid == "mix":
                        pool.wait_ge(xn_ready, L * TT + TT)
                        pool.tensor_tensor(xs[:, ms, :, :], xs[:, ms, :, :],
                                           bias[:, :].unsqueeze(1).to_broadcast([P, TT, D]),
                                           ALU.add).then_inc(bias_added, 1)
                        ln_scalars(L + 1)

        @block.tensor
        def _(pe):
            def transposes(L):
                pe.wait_ge(xhl_ready, L * 2 + 2)
                for kb in range(KB):
                    for h, src in ((HI, xh), (LO, xl)):
                        for t in range(TT):
                            last = pe.transpose(TH[kb][:, h, t * P:(t + 1) * P], src[:, t, kb * P:(kb + 1) * P],
                                                ident16[:, :])
                    last.then_inc(tr_done, 1)

            pe.wait_ge(rows_in, 5 * 16)
            pe.wait_ge(ident_ready, 2)
            pe.transpose(T[0][:, 0:NROWS], rows[:, :], ident[0:NROWS, 0:NROWS]).then_inc(rows_T, 1)

            def w_transposes(q):
                hf, kind = divmod(q, 2)
                pe.wait_ge(w_scaled, 4 * q + 4)
                if q == 0:
                    pe.wait_ge(cols_ready, 1)
                if q >= 2:
                    pe.wait_ge(bfl_ready, 2 * (q - 1))
                for kb in range(KB):
                    for i in range(4):
                        last = pe.transpose(TP[q % 2][kb][:, i * P:(i + 1) * P],
                                            wn[:, kind, 4 * hf + i, kb * P:(kb + 1) * P], ident[:, :])
                last.then_inc(w_T, 1)

            def w_folds(q):
                pe.wait_ge(bfl_ready, 2 * (q + 1))
                if q == 0:
                    pe.wait_ge(had_ready, 1)
                if q >= 2:
                    pe.wait_ge(wlo_ready, 2 * (q - 1))
                for kb in range(KB):
                    last = pe.matmul(HP[q % 2][kb][:, :], had[:, :], bfl[:, q % 2, kb, :], start=True, stop=True)
                last.then_inc(w_fold, 1)

            w_transposes(0)
            w_transposes(1)
            w_folds(0)
            w_transposes(2)
            w_folds(1)
            w_transposes(3)
            w_folds(2)
            pe.wait_ge(bfl_ready, 2 * 3)
            transposes(0)
            w_folds(3)

            def wd_transposes(r):
                if r == 0:
                    pe.wait_ge(wd_bfl, 12)
                    pe.wait_ge(bfl_ready, 2 * NG)
                if r == 2:
                    pe.wait_ge(wlo_ready, 2 * (NG - 1))
                for c in range(2):
                    for b in range(2):
                        last = pe.transpose(TWD[r][:, (2 * c + b) * P:(2 * c + b + 1) * P],
                                            wds[:, 0, b, r + 4 * c, :], ident[:, :])
                last.then_inc(wd_T, 1)

            def wd_folds(r):
                if r == 0:
                    pe.wait_ge(xTa_ready, 1)
                    pe.wait_ge(xTb_ready, 1)
                pe.wait_ge(wdT_ready, r + 1)
                pe.matmul(HWD[r][:, :], had[:, :], wdT[:, r % 2, :], start=True, stop=True).then_inc(wd_fold, 1)

            wd_transposes(0)
            wd_transposes(1)
            for r in range(4):
                if r < 2:
                    wd_transposes(r + 2)
                wd_folds(r)

            pe.wait_ge(wlo_ready, 2 * NG)

            def up_gate(K, c, fs):
                for kind, banks, freed, done in ((GATE, G, silu_ready, gate_done), (UP, U, a32_ready, up_done)):
                    if c >= 2:
                        pe.wait_ge(freed, K - 1)
                    n = 0
                    for kb in range(KB):
                        for w, h in ((HI, HI), (HI, LO), (LO, HI)):
                            mm = pe.matmul(banks[c % 2][:, :], wug[:, kind, w, kb, c * P:(c + 1) * P],
                                           xT[:, fs, h, kb, :], start=(n == 0), stop=(n == 5))
                            n += 1
                    mm.then_inc(done, 1)

            def down(K, c, J):
                pe.wait_ge(alo_ready, K + 1)
                if c == 0:
                    pe.wait_ge(x_ffn, J * TT + TT)
                for t in range(TT):
                    for n, (a, w) in enumerate(((HI, HI), (HI, LO), (LO, HI))):
                        mm = pe.matmul(Dn[t // 2][:, (t % 2) * D:(t % 2 + 1) * D], act[:, c, a, t * P:(t + 1) * P],
                                       wdn[:, c, w, :], start=(c == 0 and t % 2 == 0 and n == 0),
                                       stop=(c == NC - 1 and n == 2), skip_group_check=True)
                if c == NC - 1:
                    mm.then_inc(down_done, 1)

            def mix(ms):
                for t in range(TT):
                    n = 0
                    for kb in range(KB):
                        dst = T[t // 2][:, (t % 2) * D + kb * P:(t % 2 + 1) * D]
                        wc = slice(0, D) if kb == 0 else slice(D, D + P)
                        for a, w in ((HI, HI), (HI, LO), (LO, HI)):
                            mm = pe.matmul(dst, xT[:, ms, a, kb, t * P:(t + 1) * P], wmix[:, w, wc],
                                           start=(t % 2 == 0 and n == 0), stop=(n == 5), skip_group_check=True)
                            n += 1
                    if t % 2:
                        mm.then_inc(mix_done, 1)

            with pe.Fori(0, NIT) as it:
                for jj, (fs, mid) in enumerate(PLAN):
                    ms = 1 - fs
                    J = it * JOBS + jj
                    L = it * LNS + LN_FIRST[jj]
                    LM = L + (mid == "mix")
                    pe.wait_ge(xTa_ready, L)
                    pe.wait_ge(xTb_ready, L)
                    for c in range(NC):
                        K = it * (JOBS * NC) + jj * NC + c
                        up_gate(K, c, fs)
                        if mid == "mix" and c == 3:
                            transposes(L)
                        if mid == "mix" and c == 4:
                            pe.wait_ge(xTa_ready, L + 1)
                            pe.wait_ge(xTb_ready, L + 1)
                            if jj == 1:
                                pe.wait_ge(wmix_ready, 1)
                            mix(ms)
                        if jj == 0 and c == LAG:
                            pe.wait_ge(wdlo_ready, NC)
                        if c >= LAG:
                            down(K - LAG, c - LAG, J)
                        if c == 7:
                            transposes(LM)
                    for c in range(NC - LAG, NC):
                        down(it * (JOBS * NC) + jj * NC + c, c, J)

        @block.scalar
        def _(sc):
            def normalise(L, slot):
                sc.wait_ge(ln_small, L * 4 + 4)
                for t in range(TT):
                    sc.activation(xn[:, t, :], xs[:, slot, t, :], ACT.Identity, bias=nmr[:, t:t + 1],
                                  scale=rstd[:, t:t + 1]).then_inc(xn_ready, 1)

            def xT_block0(L, slot):
                sc.wait_ge(tr_done, L * KB + 1)
                sc.copy(xT[:, slot, :, 0, :], TH[0]).then_inc(xTa_ready, 1)

            def scale_rows(q):
                hf, kind = divmod(q, 2)
                sc.wait_ge(rinv_ready, q + 1)
                for m in range(4 * hf, 4 * hf + 4):
                    sc.activation(wn[:, kind, m, :], wn[:, kind, m, :], ACT.Copy,
                                  scale=rinv[:, NC * kind + m:NC * kind + m + 1]).then_inc(w_scaled, 1)

            def wTa_copy(q):
                sc.wait_ge(w_T, q + 1)
                if q >= 2:
                    sc.wait_ge(bfl_ready, 2 * (q - 1))
                sc.copy(wTa[:, q % 2, :], TP[q % 2][0][:, :]).then_inc(wTa_ready, 1)

            def w_hi(q):
                hf, kind = divmod(q, 2)
                sc.wait_ge(w_fold, q + 1)
                sc.wait_ge(sk_ready, 1)
                for kb in range(KB):
                    sc.activation(wug[:, kind, HI, kb, 512 * hf:512 * hf + 512], HP[q % 2][kb][:, :], ACT.Copy,
                                  scale=sk[:, kb:kb + 1]).then_inc(whi_ready, 1)

            sc.wait_ge(consts, 1)
            sc.activation(warm[:, :], mhalf[:, 0:1], ACT.Silu)
            scale_rows(0)
            scale_rows(1)
            wTa_copy(0)

            def wd_scale(b):
                sc.wait_ge(wd_in[b], 16)
                sc.wait_ge(cols_ready, 1)
                sc.activation(wds[:, 1, b], wds[:, 0, b], ACT.Copy,
                              scale=cols[:, C_WSD.start + b:C_WSD.start + b + 1]).then_inc(wd_scaled, 1)

            wd_scale(0)
            wTa_copy(1)
            wd_scale(1)
            scale_rows(2)
            w_hi(0)
            scale_rows(3)
            wTa_copy(2)
            w_hi(1)
            normalise(0, 0)
            wTa_copy(3)
            sc.wait_ge(wd_bfl, 4)
            for b, unused in enumerate((sil, a32)):
                sc.activation(unused[:, :, :].rearrange("p a s -> p (a s)"), wds[:, 0, b].rearrange("p c k -> p (c k)"),
                              ACT.Square, accum_out=wdss[:, b:b + 1]).then_inc(wd_sq, 1)
            w_hi(2)
            xT_block0(0, 0)
            w_hi(3)

            def wdT_copy(r):
                sc.wait_ge(wd_T, r + 1)
                if r >= 2:
                    sc.wait_ge(wd_fold, r - 1)
                sc.copy(wdT[:, r % 2, :], TWD[r][:, :]).then_inc(wdT_ready, 1)

            def wd_hi(r):
                sc.wait_ge(wd_fold, r + 1)
                if r == 0:
                    sc.wait_ge(feta_ready, 1)
                for c in range(2):
                    sc.activation(wdn[:, r + 4 * c, HI, :], HWD[r][:, c * D:(c + 1) * D], ACT.Copy,
                                  scale=feta[:, r + 4 * c:r + 4 * c + 1]).then_inc(wdhi_ready, 1)

            for r in range(4):
                wdT_copy(r)
            for r in range(4):
                wd_hi(r)
            sc.wait_ge(scales_ready, 1)

            with sc.Fori(0, NIT) as it:
                for jj, (fs, mid) in enumerate(PLAN):
                    ms = 1 - fs
                    L = it * LNS + LN_FIRST[jj]
                    LM = L + (mid == "mix")
                    for c in range(NC):
                        K = it * (JOBS * NC) + jj * NC + c
                        if mid == "mix" and c == 1:
                            normalise(L, ms)
                        sc.wait_ge(gate_done, K + 1)
                        if c >= 2:
                            sc.wait_ge(a32_ready, K - 1)
                        sc.activation(sil[:, c % 2, :], G[c % 2][:, :], ACT.Silu,
                                      scale=sug[:, NC + c:NC + c + 1]).then_inc(silu_ready, 1)
                        sc.wait_ge(a32_ready, K + 1)
                        sc.copy(act[:, c, HI, :], a32[:, c % 2, :]).then_inc(ahi_ready, 1)
                        if mid == "mix" and c == 3:
                            xT_block0(L, ms)
                        if c == 5:
                            normalise(LM, ms)
                        if c == 7:
                            xT_block0(LM, ms)

        @block.vector
        def _(dve):
            count = [0]

            def chained(ins):
                count[0] += 1
                ins.then_inc(dve_chain, 1)
                dve.wait_ge(dve_chain, count[0])

            dve.wait_ge(iotas, 2)
            dve.tensor_tensor(ident[:, :], rowi[:, :], coli[:, :], ALU.is_equal).then_inc(ident_ready, 1)
            dve.tensor_tensor(ident16[:, :], rowi[:, :], coli[:, :], ALU.is_equal).then_inc(ident_ready, 1)
            chained(dve.tensor_tensor(par[:, :], rowi[:, :], coli[:, :], ALU.bitwise_and))
            for s in (4, 2, 1):
                chained(dve.tensor_scalar(part[:, :], par[:, :], s, None, ALU.logical_shift_right))
                chained(dve.tensor_tensor(par[:, :], par[:, :], part[:, :], ALU.bitwise_xor))
            chained(dve.tensor_scalar(part[:, :], par[:, :], 1, None, ALU.bitwise_and))
            dve.tensor_scalar(had[:, :], part[:, :], -2.0, 1.0, ALU.mult, ALU.add).then_inc(had_ready, 1)

            def row_max(q):
                hf, kind = divmod(q, 2)
                at = NC * kind + 4 * hf
                dve.wait_ge(wn_in[q], 16)
                chained(dve.tensor_reduce(rmax[:, at:at + 4], wn[:, kind, 4 * hf:4 * hf + 4, :], AX_X, ALU.max,
                                          apply_absolute_value=True))
                chained(dve.tensor_scalar(rmax[:, at:at + 4], rmax[:, at:at + 4], TINY, None, ALU.max))
                dve.reciprocal(rinv[:, at:at + 4], rmax[:, at:at + 4]).then_inc(rinv_ready, 1)

            def butterfly(q):
                dve.wait_ge(wTa_ready, q + 1)
                if q >= 2:
                    dve.wait_ge(w_fold, q - 1)
                for kb, op in ((0, ALU.add), (1, ALU.subtract)):
                    dve.tensor_tensor(bfl[:, q % 2, kb, :], wTa[:, q % 2, :], TP[q % 2][1][:, :], op)\
                       .then_inc(bfl_ready, 1)

            def w_lo(q):
                hf, kind = divmod(q, 2)
                for kb in range(KB):
                    at = slice(512 * hf, 512 * hf + 512)
                    dve.wait_ge(whi_ready, KB * q + kb + 1)
                    dve.scalar_tensor_tensor(wug[:, kind, LO, kb, at], HP[q % 2][kb][:, :], sk[:, kb:kb + 1],
                                             wug[:, kind, HI, kb, at], ALU.mult, ALU.subtract).then_inc(wlo_ready, 1)

            def layer_stats(slot):
                for t in range(TT):
                    dve.bn_stats(stats[:, t, :], xs[:, slot, t, :]).then_inc(stats_ready, 1)

            def mean_var(L):
                dve.wait_ge(stats_ready, L * TT + TT)
                dve.sem_inc(stats_seen, 1)
                for t in range(TT):
                    dve.bn_aggr(mv[:, t, :], stats[:, t, :]).then_inc(mv_ready, 1)

            def split_rows(L):
                dve.wait_ge(xn_ready, L * TT + TT)
                dve.tensor_copy(xh[:, :, :], xn[:, :, :]).then_inc(xhl_ready, 1)
                dve.wait_ge(xhl_ready, L * 2 + 1)
                dve.tensor_tensor(xl[:, :, :], xn[:, :, :], xh[:, :, :], ALU.subtract).then_inc(xhl_ready, 1)

            def xT_block1(L, slot):
                dve.wait_ge(tr_done, L * KB + 2)
                dve.tensor_copy(xT[:, slot, :, 1, :], TH[1]).then_inc(xTb_ready, 1)

            row_max(0)
            row_max(1)
            dve.wait_ge(rows_T, 1)
            dve.tensor_copy(cols[:, :], T[0][:, 0:NROWS]).then_inc(cols_ready, 1)
            dve.wait_ge(su_in, 16)
            chained(dve.tensor_reduce(sumx[:, :], su_bc[:, :], AX_X, ALU.max, apply_absolute_value=True))
            chained(dve.tensor_scalar(sumx[:, :], sumx[:, :], TINY, None, ALU.max))
            chained(dve.reciprocal(suinv[:, :], sumx[:, :]))
            dve.wait_ge(cols_ready, 1)
            dve.tensor_scalar(sk[:, :], cols[:, C_SUG], suinv[:, 0:1], WS, ALU.mult, ALU.mult).then_inc(sk_ready, 1)
            dve.wait_ge(sk_ready, 1)
            butterfly(0)
            row_max(2)
            butterfly(1)
            row_max(3)
            dve.wait_ge(rinv_ready, NG)
            dve.wait_ge(x_in[0], 16)
            layer_stats(0)
            mean_var(0)
            w_lo(0)
            butterfly(2)
            w_lo(1)
            split_rows(0)
            butterfly(3)

            chained(dve.tensor_tensor(sug[:, :], rmax[:, :], cols[:, C_WS], ALU.mult))
            chained(dve.tensor_scalar(sug[:, :], sug[:, :], sumx[:, 0:1], 1.0 / (16.0 * XS * WS), ALU.mult, ALU.mult))
            PS_TOP = 256.0 * 16.0 * XS * WS
            chained(dve.scalar_tensor_tensor(asg[:, :], sug[:, NC:2 * NC], -1.0, sug[:, NC:2 * NC],
                                             ALU.mult, ALU.max))
            chained(dve.tensor_scalar(asg[:, :], asg[:, :], TINY, None, ALU.max))
            chained(dve.reciprocal(asgi[:, :], asg[:, :]))
            chained(dve.tensor_scalar(beta[:, :], asgi[:, :], F16_TOP / PS_TOP / PS_TOP, None, ALU.mult))
            chained(dve.scalar_tensor_tensor(fch[:, :], sug[:, 0:NC], PS_TOP * PS_TOP / F16_TOP, asg[:, :],
                                             ALU.mult, ALU.mult))
            chained(dve.tensor_tensor(fch[:, :], fch[:, :], cols[:, C_SUD], ALU.mult))
            dve.tensor_reduce(mx[:, 0:1], fch[:, :], AX_X, ALU.max, apply_absolute_value=True).then_inc(mx_ready, 1)
            dve.wait_ge(wd_sq, 2)
            dve.tensor_reduce(mx[:, 1:2], wdss[:, :], AX_X, ALU.max).then_inc(mx_ready, 1)

            w_lo(2)
            xT_block1(0, 0)

            dve.wait_ge(dg_ready, 1)
            dve.wait_ge(mix_in, 2 * 16)
            chained(dve.tensor_reduce(rpd[:, :], dg[:, :, :], AX_X, ALU.add))
            chained(dve.reciprocal(rpi[:, :], rpd[:, :]))
            chained(dve.tensor_reduce(mmx[:, :], mix_bc[:, :, :], AX_X, ALU.max, apply_absolute_value=True))
            chained(dve.tensor_scalar(msum[:, :], mmx[:, 0:1], mmx[:, 1:2], TINY, ALU.add, ALU.max))
            chained(dve.reciprocal(minv[:, :], msum[:, :]))
            chained(dve.tensor_scalar(kmix[:, :], msum[:, :], 1.0 / (MIX_TOP * XS), None, ALU.mult))
            chained(dve.tensor_scalar(rpi[:, :], rpi[:, :], minv[:, 0:1], MIX_TOP, ALU.mult, ALU.mult))
            dve.tensor_scalar(w0s[:, :], cols[:, C_W0], rpi[:, 0:1], None, ALU.mult).then_inc(mixk_ready, 1)

            dve.wait_ge(mxg_ready, 2)
            chained(dve.tensor_scalar(fall[:, :], wdnorm[:, :], NORM_MIN, mxg[:, 0:1], ALU.max, ALU.mult))
            chained(dve.tensor_scalar(fall[:, :], fall[:, :], TINY, None, ALU.max))
            chained(dve.reciprocal(finv[:, :], fall[:, :]))
            dve.tensor_scalar(feta[:, :], fch[:, :], finv[:, 0:1], F16_TOP / WD_TOP, ALU.mult, ALU.mult)\
               .then_inc(feta_ready, 1)
            dve.tensor_scalar(kdown[:, :], fall[:, :], 0.5 / 32.0 * WD_TOP / F16_TOP, None, ALU.mult)\
               .then_inc(scales_ready, 1)
            dve.wait_ge(feta_ready, 1)
            dve.wait_ge(scales_ready, 1)
            w_lo(3)
            for r in range(4):
                dve.wait_ge(wdhi_ready, 2 * r + 2)
                for c in range(2):
                    ch = r + 4 * c
                    dve.scalar_tensor_tensor(wdn[:, ch, LO, :], HWD[r][:, c * D:(c + 1) * D],
                                             feta[:, ch:ch + 1], wdn[:, ch, HI, :], ALU.mult, ALU.subtract)\
                       .then_inc(wdlo_ready, 1)

            dve.sem_inc(x_ffn, TT)
            with dve.Fori(0, NIT) as it:
                for jj, (fs, mid) in enumerate(PLAN):
                    ms = 1 - fs
                    J = it * JOBS + jj
                    L = it * LNS + LN_FIRST[jj]
                    LM = L + (mid == "mix")
                    M = it * MIXS + (jj == 2)
                    for c in range(NC):
                        K = it * (JOBS * NC) + jj * NC + c
                        if mid == "mix" and c == 0:
                            dve.wait_ge(x_ffn, J * TT + TT)
                            layer_stats(ms)
                            mean_var(L)
                        if mid == "mix" and c == 1:
                            split_rows(L)
                        if c == 6:
                            split_rows(LM)
                        dve.wait_ge(up_done, K + 1)
                        dve.wait_ge(silu_ready, K + 1)
                        dve.scalar_tensor_tensor(a32[:, c % 2, :], U[c % 2][:, :], beta[:, c:c + 1], sil[:, c % 2, :],
                                                 ALU.mult, ALU.mult).then_inc(a32_ready, 1)
                        if c == 7:
                            xT_block1(LM, ms)
                        dve.wait_ge(ahi_ready, K + 1)
                        dve.tensor_tensor(act[:, c, LO, :], a32[:, c % 2, :], act[:, c, HI, :], ALU.subtract)\
                           .then_inc(alo_ready, 1)
                        if mid == "mix" and c == 3:
                            xT_block1(L, ms)
                        if c == 4:
                            if mid == "mix":
                                dve.wait_ge(bias_added, M + 1)
                                for t in range(TT):
                                    dve.wait_ge(mix_done, M * 2 + t // 2 + 1)
                                    dve.scalar_tensor_tensor(xs[:, ms, t, :],
                                                             T[t // 2][:, (t % 2) * D:(t % 2 + 1) * D], kmix[:, 0:1],
                                                             xs[:, ms, t, :], ALU.mult, ALU.add).then_inc(x_mix, 1)
                                dve.wait_ge(x_mix, M * TT + TT)
                            elif ms == 0:
                                dve.wait_ge(x_in[0], it * 16 + 32)
                            else:
                                dve.wait_ge(x_in[1], it * 16 + 16)
                            layer_stats(ms)
                            mean_var(LM)
                    dve.wait_ge(down_done, J + 1)
                    for t in range(TT):
                        dve.scalar_tensor_tensor(xs[:, fs, t, :], Dn[t // 2][:, (t % 2) * D:(t % 2 + 1) * D],
                                                 kdown[:, 0:1], xs[:, fs, t, :], ALU.mult, ALU.add).then_inc(x_ffn, 1)


_INS = ['L0_attn_x', 'L0_attn_weight', 'L0_attn_bias', 'L0_attn_decay_value', 'L0_ffn_SU_ug', 'L0_ffn_SU_dp',
        'L0_ffn_Wscale_ug', 'L0_ffn_Wscale_dp', 'L0_ffn_W_up', 'L0_ffn_W_gate', 'L0_ffn_W_down']
_OUTS = [((16, 256, 256), 'float32')]


def kernel(**inputs):
    import numpy as _np
    import concourse.bacc as _bacc
    from concourse import mybir as _mybir
    from concourse.bass_utils import run_bass_kernel_spmd as _run

    nc = _bacc.Bacc("TRN2", target_bir_lowering=False, num_devices=1)
    arrays, args = {}, []
    for name in _INS:
        a = _np.ascontiguousarray(inputs[name])
        arrays[f"in_{name}_dram"] = a
        args.append(nc.dram_tensor(f"in_{name}_dram", a.shape, _mybir.dt.from_np(a.dtype), kind="ExternalInput").ap())
    for i, (shape, dtype) in enumerate(_OUTS):
        dt = _mybir.dt.from_np(_np.dtype(dtype))
        args.append(nc.dram_tensor(f"out_{i}_dram", shape, dt, kind="ExternalOutput").ap())
    macaron_kernel(nc, *args)
    r = _run(nc, [arrays], core_ids=[0])
    got = tuple(r.results[0][f"out_{i}_dram"] for i in range(len(_OUTS)))
    return got[0]
```

```python
from contextlib import ExitStack

import concourse.bass as bass
from concourse import mybir

ALU = mybir.AluOpType
ACT = mybir.ActivationFunctionType
F32 = mybir.dt.float32
F16 = mybir.dt.float16
I32 = mybir.dt.int32
AX_X = mybir.AxisListType.X
ABSMAX = bass.bass_isa.ReduceOp.absmax

P = 128
EPS = 1e-5
TINY = 1e-30
NORM_MIN = 1e-18

XS = 2.0 ** 10
WS = 2.0 ** 7
F16_TOP = 2.0 ** 15
MIX_TOP = 2.0 ** 14

LO_UP = 2.0 ** 11
HI, LO, HI_DN = 0, 1, 2
UP, GATE = 0, 1


def macaron_kernel(nc, x, mix_w, mix_b, decay, su_ug, su_dp, ws_ug, ws_dp, w_up, w_gate, w_down, out):
    B, E, D = x.shape
    INTER = w_up.shape[0]
    TT = 4
    SLOT = TT * P
    NIT = B * E // (2 * SLOT)
    KB = D // P
    NC = INTER // P
    NG = 4
    PIECES = [(0, 0, 2), (0, 2, 4), (1, 0, 4), (2, 0, 4), (3, 0, 4)]
    JOBS = 4
    LNS = 6
    MIXS = 2
    WD_TOP = (INTER // 4) ** 0.5
    LAG = 2

    PLAN = [(0, "load"), (1, "mix"), (0, "mix"), (1, "load")]
    LN_FIRST = [1, 2, 4, 6]

    x_d = x.rearrange("b e d -> (b e) d").rearrange("(g p t) d -> g p t d", p=P, t=TT)
    out_d = out.rearrange("b e d -> (b e) d").rearrange("(g p t) d -> g p t d", p=P, t=TT)
    w_d = {UP: w_up.rearrange("(m p) d -> p m d", p=P), GATE: w_gate.rearrange("(m p) d -> p m d", p=P)}
    wd_d = w_down.rearrange("(b p) n -> p b n", p=P)

    ctx = ExitStack()
    with ctx:
        def sb(name, shape, dt=F32):
            return ctx.enter_context(nc.sbuf_tensor(name, shape, dt))

        def sem(name):
            return ctx.enter_context(nc.semaphore(name))

        xs = sb("xs", [P, 2, TT, D])
        xn = sb("xn", [P, TT, D])
        xhl = sb("xhl", [P, 2, TT, D], F16)
        xT = sb("xT", [P, 2, 2, TT, KB, P], F16)
        act = sb("act", [P, NC, 2, SLOT], F16)
        sil = sb("sil", [P, 2, SLOT])
        a32 = sb("a32", [P, 2, SLOT])
        wug = sb("wug", [P, 2, 2, KB, INTER], F16)
        wdn = sb("wdn", [P, NC, 3, D], F16)
        wmix = sb("wmix", [P, 2, D + P], F16)
        bias = sb("bias", [P, D])
        stats = sb("stats", [P, TT, 6])
        mv = sb("mv", [P, TT, 2])
        ve = sb("ve", [P, TT])
        nmean = sb("nmean", [P, TT])
        rstd = sb("rstd", [P, TT])
        nmr = sb("nmr", [P, TT])
        mhalf = sb("mhalf", [P, TT])
        half = sb("half", [P, 1])
        warm = sb("warm", [P, 1])
        mone = sb("mone", [P, TT])
        wn = sb("wn", [P, 2, NC, D])
        wds = sb("wds", [P, 2, 2, NC, P])
        wTa = sb("wTa", [P, 2, SLOT])
        bfl = sb("bfl", [P, 2, 2, SLOT])
        wdT = sb("wdT", [P, 2, SLOT])
        rowi = sb("rowi", [P, P], I32)
        coli = sb("coli", [P, P], I32)
        par = sb("par", [P, P], I32)
        part = sb("part", [P, P], I32)
        had = sb("had", [P, P])
        ident = sb("ident", [P, P])
        NROWS = 2 * NC + KB + NC + KB + KB
        rows = sb("rows", [NROWS, P])
        cols = sb("cols", [P, NROWS])
        su_bc = sb("su_bc", [P, D])
        mix_bc = sb("mix_bc", [P, 2, D])
        dec_bc = sb("dec_bc", [P, 2])
        rmax = sb("rmax", [P, 2 * NC])
        rinv = sb("rinv", [P, 2 * NC])
        sumx = sb("sumx", [P, 1])
        suinv = sb("suinv", [P, 1])
        sk = sb("sk", [P, KB])
        sug = sb("sug", [P, 2 * NC])
        asg = sb("asg", [P, NC])
        asgi = sb("asgi", [P, NC])
        beta = sb("beta", [P, NC])
        fch = sb("fch", [P, NC])
        feta = sb("feta", [P, NC])
        mx = sb("mx", [P, 2])
        mxg = sb("mxg", [P, 2])
        wdss = sb("wdss", [P, 2])
        wdnorm = sb("wdnorm", [P, 1])
        fall = sb("fall", [P, 1])
        finv = sb("finv", [P, 1])
        kdown = sb("kdown", [P, 1])
        pw = sb("pw", [P, 9, 2])
        rp = sb("rp", [P, 2, D])
        dg = sb("dg", [P, 2, P])
        rpd = sb("rpd", [P, 2])
        rpi = sb("rpi", [P, 2])
        mmx = sb("mmx", [P, 2])
        msum = sb("msum", [P, 1])
        minv = sb("minv", [P, 1])
        kmix = sb("kmix", [P, 1])
        w0s = sb("w0s", [P, KB])
        mxa = sb("mxa", [P, D + P])
        mxb = sb("mxb", [P, D + P])
        mxc = sb("mxc", [P, D + P])

        C_WS = slice(0, 2 * NC)
        C_SUG = slice(2 * NC, 2 * NC + KB)
        C_SUD = slice(2 * NC + KB, 3 * NC + KB)
        C_WSD = slice(3 * NC + KB, 3 * NC + 2 * KB)
        C_W0 = slice(3 * NC + 2 * KB, 3 * NC + 3 * KB)

        G = [ctx.enter_context(nc.psum_tensor(f"G{i}", [P, 512], F32)) for i in range(2)]
        U = [ctx.enter_context(nc.psum_tensor(f"U{i}", [P, 512], F32)) for i in range(2)]
        Dn = [ctx.enter_context(nc.psum_tensor(f"Dn{i}", [P, 512], F32)) for i in range(2)]
        T = [ctx.enter_context(nc.psum_tensor(f"T{i}", [P, 512], F32)) for i in range(2)]
        TP = [T, Dn]
        HP = [G, U]
        TWD = [Dn[0], Dn[1], G[0], G[1]]
        HWD = [T[0], T[1], Dn[0], Dn[1]]

        wn_in = [sem(f"wn_in{i}") for i in range(len(PIECES))]
        wd_in = [sem(f"wd_in{b}") for b in range(2)]
        rows_in = sem("rows_in")
        dec_in = sem("dec_in")
        su_in = sem("su_in")
        mix_in = sem("mix_in")
        x_in = [sem("x_in0"), sem("x_in1")]
        x_out = [sem("x_out0"), sem("x_out1")]
        xT_in = sem("xT_in")
        xhl_seen = sem("xhl_seen")
        iotas = sem("iotas")
        consts = sem("consts")
        had_ready = sem("had_ready")
        ident_ready = sem("ident_ready")
        rows_T = sem("rows_T")
        cols_ready = sem("cols_ready")
        sk_ready = sem("sk_ready")
        rinv_ready = sem("rinv_ready")
        w_scaled = sem("w_scaled")
        w_T = sem("w_T")
        wTa_ready = sem("wTa_ready")
        bfl_ready = sem("bfl_ready")
        w_fold = sem("w_fold")
        whi_ready = sem("whi_ready")
        wlo_ready = sem("wlo_ready")
        mx_ready = sem("mx_ready")
        mxg_ready = sem("mxg_ready")
        wd_scaled = sem("wd_scaled")
        wd_sq = sem("wd_sq")
        wd_bfl = sem("wd_bfl")
        wd_bfl_v = sem("wd_bfl_v")
        wd_T = sem("wd_T")
        wdT_ready = sem("wdT_ready")
        wd_fold = sem("wd_fold")
        feta_ready = sem("feta_ready")
        wdhi_ready = sem("wdhi_ready")
        wdlo_ready = sem("wdlo_ready")
        scales_ready = sem("scales_ready")
        pow_chain = sem("pow_chain")
        dg_ready = sem("dg_ready")
        mixk_ready = sem("mixk_ready")
        mix_chain = sem("mix_chain")
        wmix_ready = sem("wmix_ready")
        dve_chain = sem("dve_chain")

        gate_done = sem("gate_done")
        up_done = sem("up_done")
        down_done = sem("down_done")
        mix_done = sem("mix_done")
        silu_ready = sem("silu_ready")
        ahi_ready = sem("ahi_ready")
        xn_ready = sem("xn_ready")
        a32_ready = sem("a32_ready")
        alo_ready = sem("alo_ready")
        x_ffn = sem("x_ffn")
        x_mix = sem("x_mix")
        stats_ready = sem("stats_ready")
        mv_ready = sem("mv_ready")
        xhl_ready = sem("xhl_ready")
        stats_seen = sem("stats_seen")
        ln_small = sem("ln_small")
        bias_added = sem("bias_added")

        def wd_butterfly(eng, s, b, done):
            src = wds[:, (s + 1) % 2, b].rearrange("p (g a h) k -> p g a (h k)", a=2, h=1 << s)
            dst = wds[:, s % 2, b].rearrange("p (g a h) k -> p g a (h k)", a=2, h=1 << s)
            for a, op in enumerate((ALU.add, ALU.subtract)):
                eng.tensor_tensor(dst[:, :, a], src[:, :, 0], src[:, :, 1], op).then_inc(done, 1)

        block = ctx.enter_context(nc.Block())

        @block.sync
        def _(sp):
            def load_w(i):
                q, m0, m1 = PIECES[i]
                hf, kind = divmod(q, 2)
                at = slice(4 * hf + m0, 4 * hf + m1)
                sp.dma_start(wn[:, kind, at, :], w_d[kind][:, at, :]).then_inc(wn_in[i], 16)

            def load_wd(b):
                sp.dma_start(wds[:, 0, b].rearrange("p c k -> p (c k)"), wd_d[:, b, :]).then_inc(wd_in[b], 16)

            load_w(0)
            load_w(1)
            sp.dma_start(rows[0:2 * NC, :], ws_ug.rearrange("(r c) -> r c", c=P)).then_inc(rows_in, 16)
            sp.dma_start(rows[C_SUG, :], su_ug.rearrange("(r c) -> r c", c=P)).then_inc(rows_in, 16)
            load_w(2)
            sp.dma_start(rows[C_SUD, :], su_dp.rearrange("(r c) -> r c", c=P)).then_inc(rows_in, 16)
            sp.dma_start(rows[C_WSD, :], ws_dp.rearrange("(r c) -> r c", c=P)).then_inc(rows_in, 16)
            sp.dma_start(rows[C_W0, :], mix_w[0:1, :].rearrange("a (r c) -> (a r) c", c=P)).then_inc(rows_in, 16)
            sp.dma_start(dec_bc[:, :], decay.rearrange("a o -> o a").to_broadcast([P, 2])).then_inc(dec_in, 16)
            load_wd(0)
            sp.dma_start(su_bc[:, :], su_ug.rearrange("(a d) -> a d", a=1).to_broadcast([P, D])).then_inc(su_in, 16)
            load_wd(1)
            load_w(3)
            load_w(4)
            sp.dma_start(xs[:, 0, :, :], x_d[0]).then_inc(x_in[0], 16)
            sp.dma_start(mix_bc[:, :, :].rearrange("p a d -> p (a d)"),
                         mix_w.rearrange("(o a) d -> o (a d)", o=1).to_broadcast([P, 2 * D])).then_inc(mix_in, 16)
            sp.dma_start(bias[:, :], mix_b.rearrange("(a d) -> a d", a=1).to_broadcast([P, D])).then_inc(mix_in, 16)

            def transpose_rows(L, slot):
                for h in (HI, LO):
                    sp.wait_ge(xhl_ready, L * 2 + h + 1)
                    sp.sem_inc(xhl_seen, 1)
                    sp.dma_start_transpose(xT[:, slot, h].rearrange("p t k s -> p (t k) s"),
                                           xhl[:, h].rearrange("p t d -> p (t d)")).then_inc(xT_in, 16)

            def store(group, slot, before):
                for t in range(0, TT, 2):
                    sp.wait_ge(x_ffn, before + t + 2)
                    sp.dma_start(out_d[group][:, t:t + 2, :], xs[:, slot, t:t + 2, :]).then_inc(x_out[slot], 16)

            sp.sem_inc(x_out[1], 32)
            transpose_rows(0, 0)
            with sp.Fori(0, NIT) as it:
                sp.wait_ge(x_out[1], it * 32 + 32)
                sp.dma_start(xs[:, 1, :, :], x_d[it * 2 + 1]).then_inc(x_in[1], 16)
                transpose_rows(it * LNS + 1, 1)
                for i in range(2 * MIXS):
                    transpose_rows(it * LNS + 2 + i, i // 2)
                store(it * 2, 0, it * (JOBS * TT) + 3 * TT)
                sp.wait_ge(x_out[0], it * 32 + 32)
                sp.dma_start(xs[:, 0, :, :], x_d[((it + 1) % NIT) * 2]).then_inc(x_in[0], 16)
                transpose_rows(it * LNS + 6, 0)
                store(it * 2 + 1, 1, it * (JOBS * TT) + 4 * TT)
            sp.wait_ge(xT_in, 2 * 16 * (LNS * NIT + 1))
            sp.wait_ge(x_out[0], 32 * NIT)
            sp.wait_ge(x_out[1], 32 * NIT + 32)

        @block.gpsimd
        def _(pool):
            pool.iota(rowi[:, :], [[0, P]], base=0, channel_multiplier=1).then_inc(iotas, 1)
            pool.iota(coli[:, :], [[1, P]], base=0, channel_multiplier=0).then_inc(iotas, 1)
            pool.memset(mhalf[:, :], -0.5).then_inc(consts, 1)
            pool.memset(mone[:, :], -1.0).then_inc(consts, 1)
            pool.memset(half[:, :], 0.5).then_inc(consts, 1)

            def ln_scalars(L):
                pool.wait_ge(mv_ready, L * TT + TT)
                pool.tensor_tensor(nmean[:, :], mv[:, :, 0], mone[:, :], ALU.mult).then_inc(ln_small, 1)
                pool.tensor_scalar(ve[:, :], mv[:, :, 1], EPS, 1.0 / (XS * XS), ALU.add, ALU.mult)\
                    .then_inc(ln_small, 1)
                pool.wait_ge(ln_small, L * 4 + 2)
                pool.tensor_tensor(rstd[:, :], ve[:, :], mhalf[:, :], ALU.pow).then_inc(ln_small, 1)
                pool.wait_ge(ln_small, L * 4 + 3)
                pool.tensor_tensor(nmr[:, :], nmean[:, :], rstd[:, :], ALU.mult).then_inc(ln_small, 1)

            pool.wait_ge(consts, 3)
            pool.wait_ge(dec_in, 16)
            pool.tensor_scalar(pw[:, 0, :], dec_bc[:, :], 0.9, 1.0, ALU.max, ALU.min).then_inc(pow_chain, 1)
            pool.memset(rp[:, :, 0:1], 1.0).then_inc(pow_chain, 1)
            for k in range(8):
                n = 1 << k
                pool.wait_ge(pow_chain, 2 * k + 2)
                pool.tensor_tensor(rp[:, :, n:2 * n], rp[:, :, 0:n],
                                   pw[:, k, :].unsqueeze(2).to_broadcast([P, 2, n]), ALU.mult).then_inc(pow_chain, 1)
                pool.tensor_tensor(pw[:, k + 1, :], pw[:, k, :], pw[:, k, :], ALU.mult).then_inc(pow_chain, 1)
            pool.wait_ge(pow_chain, 18)
            pool.wait_ge(ident_ready, 1)
            pool.tensor_tensor(dg[:, :, :], rp[:, :, 0:P], ident[:, :].unsqueeze(1).to_broadcast([P, 2, P]),
                               ALU.mult).then_inc(dg_ready, 1)

            for b in range(2):
                pool.wait_ge(wd_scaled, b + 1)
                wd_butterfly(pool, 0, b, wd_bfl)
            pool.wait_ge(wd_bfl, 2)
            wd_butterfly(pool, 1, 0, wd_bfl)
            ln_scalars(0)
            pool.wait_ge(wd_bfl, 4)
            wd_butterfly(pool, 1, 1, wd_bfl)
            pool.wait_ge(wd_bfl, 6)
            wd_butterfly(pool, 2, 0, wd_bfl)
            pool.wait_ge(mx_ready, 2)
            pool.partition_all_reduce(mxg[:, :], mx[:, :], P, ABSMAX).then_inc(mxg_ready, 1)
            pool.wait_ge(mxg_ready, 1)
            pool.tensor_tensor(wdnorm[:, :], mxg[:, 1:2], half[:, :], ALU.pow).then_inc(mxg_ready, 1)

            pool.wait_ge(mixk_ready, 1)
            pool.tensor_scalar(mxa[:, 0:D], rp[:, 0, :], w0s[:, 0:1], None, ALU.mult).then_inc(mix_chain, 1)
            pool.tensor_scalar(mxa[:, D:D + P], rp[:, 0, 0:P], w0s[:, 1:2], None, ALU.mult).then_inc(mix_chain, 1)
            pool.tensor_tensor(mxb[:, 0:D], rp[:, 1, :], mix_bc[:, 1, :], ALU.mult).then_inc(mix_chain, 1)
            pool.tensor_tensor(mxb[:, D:D + P], rp[:, 1, 0:P], mix_bc[:, 1, P:D], ALU.mult).then_inc(mix_chain, 1)
            pool.wait_ge(mix_chain, 4)
            pool.tensor_scalar(mxc[:, :], mxb[:, :], rpi[:, 1:2], None, ALU.mult).then_inc(mix_chain, 1)
            pool.wait_ge(mix_chain, 5)
            pool.tensor_tensor(mxb[:, :], mxa[:, :], mxc[:, :], ALU.add).then_inc(mix_chain, 1)
            pool.wait_ge(mix_chain, 6)
            pool.affine_select(out=mxa[:, 0:D], in_=mxb[:, 0:D], compare_op=ALU.is_ge, fill=0.0, base=0,
                               pattern=[[1, D]], channel_multiplier=-1).then_inc(mix_chain, 1)
            pool.affine_select(out=mxa[:, D:D + P], in_=mxb[:, D:D + P], compare_op=ALU.is_ge, fill=0.0, base=0,
                               pattern=[[1, P]], channel_multiplier=-1).then_inc(mix_chain, 1)
            pool.wait_ge(mix_chain, 8)
            pool.tensor_copy(wmix[:, HI, :], mxa[:, :]).then_inc(mix_chain, 1)
            pool.wait_ge(mix_chain, 9)
            pool.tensor_tensor(wmix[:, LO, :], mxa[:, :], wmix[:, HI, :], ALU.subtract).then_inc(wmix_ready, 1)

            with pool.Fori(0, NIT) as it:
                for jj, (fs, mid) in enumerate(PLAN):
                    ms = 1 - fs
                    L = it * LNS + LN_FIRST[jj]
                    ln_scalars(L)
                    if mid == "mix":
                        pool.wait_ge(xn_ready, L * TT + TT)
                        pool.tensor_tensor(xs[:, ms, :, :], xs[:, ms, :, :],
                                           bias[:, :].unsqueeze(1).to_broadcast([P, TT, D]),
                                           ALU.add).then_inc(bias_added, 1)
                        ln_scalars(L + 1)

        @block.tensor
        def _(pe):
            pe.wait_ge(rows_in, 5 * 16)
            pe.wait_ge(ident_ready, 1)
            pe.transpose(G[0][:, 0:NROWS], rows[:, :], ident[0:NROWS, 0:NROWS]).then_inc(rows_T, 1)

            def w_transposes(q):
                hf, kind = divmod(q, 2)
                pe.wait_ge(w_scaled, 4 * q + 4)
                if q >= 2:
                    pe.wait_ge(bfl_ready, 2 * (q - 1))
                for kb in range(KB):
                    for i in range(4):
                        last = pe.transpose(TP[q % 2][kb][:, i * P:(i + 1) * P],
                                            wn[:, kind, 4 * hf + i, kb * P:(kb + 1) * P], ident[:, :])
                last.then_inc(w_T, 1)

            def w_folds(q):
                pe.wait_ge(bfl_ready, 2 * (q + 1))
                if q == 0:
                    pe.wait_ge(had_ready, 1)
                    pe.wait_ge(cols_ready, 1)
                if q >= 2:
                    pe.wait_ge(wlo_ready, 2 * (q - 1))
                for kb in range(KB):
                    last = pe.matmul(HP[q % 2][kb][:, :], had[:, :], bfl[:, q % 2, kb, :], start=True, stop=True)
                last.then_inc(w_fold, 1)

            w_transposes(0)
            w_transposes(1)
            w_folds(0)
            w_transposes(2)
            w_folds(1)
            w_transposes(3)
            w_folds(2)
            w_folds(3)

            def wd_transposes(r):
                if r == 0:
                    pe.wait_ge(wd_bfl, 10)
                    pe.wait_ge(wd_bfl_v, 2)
                    pe.wait_ge(bfl_ready, 2 * NG)
                if r == 2:
                    pe.wait_ge(wlo_ready, 2 * (NG - 1))
                for c in range(2):
                    for b in range(2):
                        last = pe.transpose(TWD[r][:, (2 * c + b) * P:(2 * c + b + 1) * P],
                                            wds[:, 0, b, r + 4 * c, :], ident[:, :])
                last.then_inc(wd_T, 1)

            def wd_folds(r):
                pe.wait_ge(wdT_ready, r + 1)
                pe.matmul(HWD[r][:, :], had[:, :], wdT[:, r % 2, :], start=True, stop=True).then_inc(wd_fold, 1)

            wd_transposes(0)
            wd_transposes(1)
            for r in range(4):
                if r < 2:
                    wd_transposes(r + 2)
                wd_folds(r)

            pe.wait_ge(wlo_ready, 2 * NG)

            def up_gate(K, c, fs):
                for kind, banks, freed, done in ((GATE, G, silu_ready, gate_done), (UP, U, a32_ready, up_done)):
                    if c >= 2:
                        pe.wait_ge(freed, K - 1)
                    n = 0
                    for kb in range(KB):
                        for w, h in ((HI, HI), (HI, LO), (LO, HI)):
                            mm = pe.matmul(banks[c % 2][:, :], wug[:, kind, w, kb, c * P:(c + 1) * P],
                                           xT[:, fs, h, :, kb, :], start=(n == 0), stop=(n == 5))
                            n += 1
                    mm.then_inc(done, 1)

            def down(K, c, J):
                pe.wait_ge(alo_ready, K + 1)
                if c == 0:
                    pe.wait_ge(x_ffn, J * TT + TT)
                for t in range(TT):
                    for n, (a, w) in enumerate(((HI, HI), (HI, LO), (LO, HI_DN))):
                        mm = pe.matmul(Dn[t // 2][:, (t % 2) * D:(t % 2 + 1) * D], act[:, c, a, t * P:(t + 1) * P],
                                       wdn[:, c, w, :], start=(c == 0 and t % 2 == 0 and n == 0),
                                       stop=(c == NC - 1 and n == 2), skip_group_check=True)
                    if c == NC - 1 and t % 2:
                        mm.then_inc(down_done, 1)

            def mix(ms):
                for t in range(TT):
                    n = 0
                    for kb in range(KB):
                        dst = T[t // 2][:, (t % 2) * D + kb * P:(t % 2 + 1) * D]
                        wc = slice(0, D) if kb == 0 else slice(D, D + P)
                        for a, w in ((HI, HI), (HI, LO), (LO, HI)):
                            mm = pe.matmul(dst, xT[:, ms, a, t, kb, :], wmix[:, w, wc],
                                           start=(t % 2 == 0 and n == 0), stop=(n == 5), skip_group_check=True)
                            n += 1
                    if t % 2:
                        mm.then_inc(mix_done, 1)

            with pe.Fori(0, NIT) as it:
                for jj, (fs, mid) in enumerate(PLAN):
                    ms = 1 - fs
                    J = it * JOBS + jj
                    L = it * LNS + LN_FIRST[jj]
                    pe.wait_ge(xT_in, L * 32)
                    for c in range(NC):
                        K = it * (JOBS * NC) + jj * NC + c
                        up_gate(K, c, fs)
                        if mid == "mix" and c == 4:
                            pe.wait_ge(xT_in, L * 32 + 32)
                            if jj == 1:
                                pe.wait_ge(wmix_ready, 1)
                            mix(ms)
                        if jj == 0 and c == LAG:
                            pe.wait_ge(wdlo_ready, NC + 1)
                        if c >= LAG:
                            down(K - LAG, c - LAG, J)
                    for c in range(NC - LAG, NC):
                        down(it * (JOBS * NC) + jj * NC + c, c, J)

        @block.scalar
        def _(sc):
            def normalise(L, slot):
                sc.wait_ge(ln_small, L * 4 + 4)
                for t in range(TT):
                    sc.activation(xn[:, t, :], xs[:, slot, t, :], ACT.Identity, bias=nmr[:, t:t + 1],
                                  scale=rstd[:, t:t + 1]).then_inc(xn_ready, 1)

            def scale_rows(i):
                q, m0, m1 = PIECES[i]
                hf, kind = divmod(q, 2)
                sc.wait_ge(rinv_ready, i + 1)
                for m in range(4 * hf + m0, 4 * hf + m1):
                    sc.activation(wn[:, kind, m, :], wn[:, kind, m, :], ACT.Copy,
                                  scale=rinv[:, NC * kind + m:NC * kind + m + 1]).then_inc(w_scaled, 1)

            def wTa_copy(q):
                sc.wait_ge(w_T, q + 1)
                if q >= 2:
                    sc.wait_ge(bfl_ready, 2 * (q - 1))
                sc.copy(wTa[:, q % 2, :], TP[q % 2][0][:, :]).then_inc(wTa_ready, 1)

            def w_hi(q):
                hf, kind = divmod(q, 2)
                sc.wait_ge(w_fold, q + 1)
                sc.wait_ge(sk_ready, 1)
                for kb in range(KB):
                    sc.activation(wug[:, kind, HI, kb, 512 * hf:512 * hf + 512], HP[q % 2][kb][:, :], ACT.Copy,
                                  scale=sk[:, kb:kb + 1]).then_inc(whi_ready, 1)

            sc.wait_ge(consts, 1)
            sc.activation(warm[:, :], mhalf[:, 0:1], ACT.Silu)
            scale_rows(0)
            scale_rows(1)
            wTa_copy(0)
            scale_rows(2)

            def wd_scale(b):
                sc.wait_ge(wd_in[b], 16)
                sc.wait_ge(cols_ready, 1)
                sc.activation(wds[:, 1, b], wds[:, 0, b], ACT.Copy,
                              scale=cols[:, C_WSD.start + b:C_WSD.start + b + 1]).then_inc(wd_scaled, 1)

            wd_scale(0)
            wTa_copy(1)
            wd_scale(1)
            scale_rows(3)
            w_hi(0)
            scale_rows(4)
            wTa_copy(2)
            w_hi(1)
            wTa_copy(3)
            normalise(0, 0)
            w_hi(2)
            sc.wait_ge(wd_bfl, 8)
            for b, unused in enumerate((sil, a32)):
                sc.activation(unused[:, :, :].rearrange("p a s -> p (a s)"), wds[:, 1, b].rearrange("p c k -> p (c k)"),
                              ACT.Square, accum_out=wdss[:, b:b + 1]).then_inc(wd_sq, 1)
            w_hi(3)

            def wdT_copy(r):
                sc.wait_ge(wd_T, r + 1)
                if r >= 2:
                    sc.wait_ge(wd_fold, r - 1)
                sc.copy(wdT[:, r % 2, :], TWD[r][:, :]).then_inc(wdT_ready, 1)

            def wd_hi(r):
                sc.wait_ge(wd_fold, r + 1)
                if r == 0:
                    sc.wait_ge(feta_ready, 1)
                for c in range(2):
                    sc.activation(wdn[:, r + 4 * c, HI, :], HWD[r][:, c * D:(c + 1) * D], ACT.Copy,
                                  scale=feta[:, r + 4 * c:r + 4 * c + 1]).then_inc(wdhi_ready, 1)

            for r in range(4):
                wdT_copy(r)
            for r in range(4):
                wd_hi(r)
            sc.wait_ge(scales_ready, 1)

            with sc.Fori(0, NIT) as it:
                for jj, (fs, mid) in enumerate(PLAN):
                    ms = 1 - fs
                    L = it * LNS + LN_FIRST[jj]
                    LM = L + (mid == "mix")
                    for c in range(NC):
                        K = it * (JOBS * NC) + jj * NC + c
                        if mid == "mix" and c == 1:
                            normalise(L, ms)
                        sc.wait_ge(gate_done, K + 1)
                        if c >= 2:
                            sc.wait_ge(a32_ready, K - 1)
                        sc.activation(sil[:, c % 2, :], G[c % 2][:, :], ACT.Silu,
                                      scale=sug[:, NC + c:NC + c + 1]).then_inc(silu_ready, 1)
                        sc.wait_ge(a32_ready, K + 1)
                        sc.activation(act[:, c, HI, :], a32[:, c % 2, :], ACT.Copy, scale=1.0 / LO_UP)\
                          .then_inc(ahi_ready, 1)
                        if c == 5:
                            normalise(LM, ms)

        @block.vector
        def _(dve):
            count = [0]

            def chained(*steps):
                count[0] += len(steps)
                for ins in steps:
                    ins.then_inc(dve_chain, 1)
                dve.wait_ge(dve_chain, count[0])

            dve.wait_ge(iotas, 2)
            dve.tensor_tensor(ident[:, :], rowi[:, :], coli[:, :], ALU.is_equal).then_inc(ident_ready, 1)
            chained(dve.tensor_tensor(par[:, :], rowi[:, :], coli[:, :], ALU.bitwise_and))

            def parity_step(s):
                chained(dve.tensor_scalar(part[:, :], par[:, :], s, None, ALU.logical_shift_right))
                chained(dve.tensor_tensor(par[:, :], par[:, :], part[:, :], ALU.bitwise_xor))

            def row_max(i):
                q, m0, m1 = PIECES[i]
                hf, kind = divmod(q, 2)
                at = slice(NC * kind + 4 * hf + m0, NC * kind + 4 * hf + m1)
                dve.wait_ge(wn_in[i], 16)
                chained(dve.tensor_reduce(rmax[:, at], wn[:, kind, 4 * hf + m0:4 * hf + m1, :], AX_X, ALU.max,
                                          apply_absolute_value=True))
                chained(dve.tensor_scalar(rmax[:, at], rmax[:, at], TINY, None, ALU.max))
                dve.reciprocal(rinv[:, at], rmax[:, at]).then_inc(rinv_ready, 1)

            def butterfly(q):
                dve.wait_ge(wTa_ready, q + 1)
                if q >= 2:
                    dve.wait_ge(w_fold, q - 1)
                for kb, op in ((0, ALU.add), (1, ALU.subtract)):
                    dve.tensor_tensor(bfl[:, q % 2, kb, :], wTa[:, q % 2, :], TP[q % 2][1][:, :], op)\
                       .then_inc(bfl_ready, 1)

            def w_lo(q):
                hf, kind = divmod(q, 2)
                for kb in range(KB):
                    at = slice(512 * hf, 512 * hf + 512)
                    dve.wait_ge(whi_ready, KB * q + kb + 1)
                    dve.scalar_tensor_tensor(wug[:, kind, LO, kb, at], HP[q % 2][kb][:, :], sk[:, kb:kb + 1],
                                             wug[:, kind, HI, kb, at], ALU.mult, ALU.subtract).then_inc(wlo_ready, 1)

            def layer_stats(slot):
                for t in range(TT):
                    dve.bn_stats(stats[:, t, :], xs[:, slot, t, :]).then_inc(stats_ready, 1)

            def mean_var(L):
                dve.wait_ge(stats_ready, L * TT + TT)
                dve.sem_inc(stats_seen, 1)
                for t in range(TT):
                    dve.bn_aggr(mv[:, t, :], stats[:, t, :]).then_inc(mv_ready, 1)

            def split_hi(L):
                dve.wait_ge(xn_ready, L * TT + TT)
                dve.tensor_copy(xhl[:, HI], xn[:, :, :]).then_inc(xhl_ready, 1)

            def split_lo(L):
                dve.wait_ge(xhl_ready, L * 2 + 1)
                dve.tensor_tensor(xhl[:, LO], xn[:, :, :], xhl[:, HI], ALU.subtract).then_inc(xhl_ready, 1)

            parity_step(4)
            row_max(0)
            row_max(1)
            parity_step(2)
            parity_step(1)
            chained(dve.tensor_scalar(part[:, :], par[:, :], 1, None, ALU.bitwise_and))
            dve.tensor_scalar(had[:, :], part[:, :], -2.0, 1.0, ALU.mult, ALU.add).then_inc(had_ready, 1)
            row_max(2)
            dve.wait_ge(rows_T, 1)
            dve.tensor_copy(cols[:, :], G[0][:, 0:NROWS]).then_inc(cols_ready, 1)
            butterfly(0)
            dve.wait_ge(su_in, 16)
            chained(dve.tensor_reduce(sumx[:, :], su_bc[:, :], AX_X, ALU.max, apply_absolute_value=True))
            chained(dve.tensor_scalar(sumx[:, :], sumx[:, :], TINY, None, ALU.max))
            chained(dve.reciprocal(suinv[:, :], sumx[:, :]))
            dve.wait_ge(cols_ready, 1)
            dve.tensor_scalar(sk[:, :], cols[:, C_SUG], suinv[:, 0:1], WS, ALU.mult, ALU.mult).then_inc(sk_ready, 1)
            dve.wait_ge(sk_ready, 1)
            row_max(3)
            butterfly(1)
            row_max(4)
            dve.wait_ge(rinv_ready, len(PIECES))
            dve.wait_ge(x_in[0], 16)
            layer_stats(0)
            mean_var(0)
            w_lo(0)
            butterfly(2)
            w_lo(1)
            butterfly(3)
            split_hi(0)
            split_lo(0)
            dve.wait_ge(wd_bfl, 8)
            wd_butterfly(dve, 2, 1, wd_bfl_v)
            w_lo(2)

            PS_TOP = 256.0 * 16.0 * XS * WS
            dve.wait_ge(dg_ready, 1)
            dve.wait_ge(mix_in, 2 * 16)
            chained(dve.tensor_tensor(sug[:, :], rmax[:, :], cols[:, C_WS], ALU.mult),
                    dve.tensor_reduce(rpd[:, :], dg[:, :, :], AX_X, ALU.add),
                    dve.tensor_reduce(mmx[:, :], mix_bc[:, :, :], AX_X, ALU.max, apply_absolute_value=True))
            chained(dve.tensor_scalar(sug[:, :], sug[:, :], sumx[:, 0:1], 1.0 / (16.0 * XS * WS), ALU.mult, ALU.mult),
                    dve.reciprocal(rpi[:, :], rpd[:, :]),
                    dve.tensor_scalar(msum[:, :], mmx[:, 0:1], mmx[:, 1:2], TINY, ALU.add, ALU.max))
            chained(dve.scalar_tensor_tensor(asg[:, :], sug[:, NC:2 * NC], -1.0, sug[:, NC:2 * NC],
                                             ALU.mult, ALU.max),
                    dve.reciprocal(minv[:, :], msum[:, :]),
                    dve.tensor_scalar(kmix[:, :], msum[:, :], 1.0 / (MIX_TOP * XS), None, ALU.mult))
            chained(dve.tensor_scalar(asg[:, :], asg[:, :], TINY, None, ALU.max),
                    dve.tensor_scalar(rpi[:, :], rpi[:, :], minv[:, 0:1], MIX_TOP, ALU.mult, ALU.mult))
            dve.tensor_scalar(w0s[:, :], cols[:, C_W0], rpi[:, 0:1], None, ALU.mult).then_inc(mixk_ready, 1)
            chained(dve.reciprocal(asgi[:, :], asg[:, :]),
                    dve.scalar_tensor_tensor(fch[:, :], sug[:, 0:NC], PS_TOP * PS_TOP / F16_TOP, asg[:, :],
                                             ALU.mult, ALU.mult))
            chained(dve.tensor_scalar(beta[:, :], asgi[:, :], LO_UP * F16_TOP / PS_TOP / PS_TOP, None, ALU.mult),
                    dve.tensor_tensor(fch[:, :], fch[:, :], cols[:, C_SUD], ALU.mult))
            dve.tensor_reduce(mx[:, 0:1], fch[:, :], AX_X, ALU.max, apply_absolute_value=True).then_inc(mx_ready, 1)
            dve.wait_ge(wd_sq, 2)
            dve.tensor_reduce(mx[:, 1:2], wdss[:, :], AX_X, ALU.max).then_inc(mx_ready, 1)
            w_lo(3)
            dve.wait_ge(mxg_ready, 2)
            chained(dve.tensor_scalar(fall[:, :], wdnorm[:, :], NORM_MIN, mxg[:, 0:1], ALU.max, ALU.mult))
            chained(dve.tensor_scalar(fall[:, :], fall[:, :], TINY, None, ALU.max))
            chained(dve.reciprocal(finv[:, :], fall[:, :]))
            dve.tensor_scalar(feta[:, :], fch[:, :], finv[:, 0:1], F16_TOP / WD_TOP, ALU.mult, ALU.mult)\
               .then_inc(feta_ready, 1)
            dve.tensor_scalar(kdown[:, :], fall[:, :], 0.5 / 32.0 * WD_TOP / F16_TOP, None, ALU.mult)\
               .then_inc(scales_ready, 1)
            dve.wait_ge(feta_ready, 1)
            dve.wait_ge(scales_ready, 1)
            for r in range(4):
                dve.wait_ge(wdhi_ready, 2 * r + 2)
                for c in range(2):
                    ch = r + 4 * c
                    dve.scalar_tensor_tensor(wdn[:, ch, LO, :], HWD[r][:, c * D:(c + 1) * D],
                                             feta[:, ch:ch + 1], wdn[:, ch, HI, :], ALU.mult, ALU.subtract)\
                       .then_inc(wdlo_ready, 1)

            dve.wait_ge(wdhi_ready, NC)
            dve.tensor_scalar(wdn[:, :, HI_DN, :], wdn[:, :, HI, :], 1.0 / LO_UP, None, ALU.mult)\
               .then_inc(wdlo_ready, 1)

            dve.sem_inc(x_ffn, TT)
            with dve.Fori(0, NIT) as it:
                for jj, (fs, mid) in enumerate(PLAN):
                    ms = 1 - fs
                    J = it * JOBS + jj
                    L = it * LNS + LN_FIRST[jj]
                    LM = L + (mid == "mix")
                    M = it * MIXS + (jj == 2)
                    for c in range(NC):
                        K = it * (JOBS * NC) + jj * NC + c
                        if mid == "mix" and c == 0:
                            dve.wait_ge(x_ffn, J * TT + TT)
                            layer_stats(ms)
                            mean_var(L)
                        if mid == "mix" and c == 1:
                            split_hi(L)
                        if c == 6:
                            split_hi(LM)
                        dve.wait_ge(up_done, K + 1)
                        dve.wait_ge(silu_ready, K + 1)
                        dve.scalar_tensor_tensor(a32[:, c % 2, :], U[c % 2][:, :], beta[:, c:c + 1], sil[:, c % 2, :],
                                                 ALU.mult, ALU.mult).then_inc(a32_ready, 1)
                        if mid == "mix" and c == 1:
                            split_lo(L)
                        if c == 6:
                            split_lo(LM)
                        dve.wait_ge(ahi_ready, K + 1)
                        dve.scalar_tensor_tensor(act[:, c, LO, :], act[:, c, HI, :], -LO_UP, a32[:, c % 2, :],
                                                 ALU.mult, ALU.add).then_inc(alo_ready, 1)
                        if c == 4:
                            if mid == "mix":
                                dve.wait_ge(bias_added, M + 1)
                                for t in range(TT):
                                    dve.wait_ge(mix_done, M * 2 + t // 2 + 1)
                                    dve.scalar_tensor_tensor(xs[:, ms, t, :],
                                                             T[t // 2][:, (t % 2) * D:(t % 2 + 1) * D], kmix[:, 0:1],
                                                             xs[:, ms, t, :], ALU.mult, ALU.add).then_inc(x_mix, 1)
                                dve.wait_ge(x_mix, M * TT + TT)
                            elif ms == 0:
                                dve.wait_ge(x_in[0], it * 16 + 32)
                            else:
                                dve.wait_ge(x_in[1], it * 16 + 16)
                            layer_stats(ms)
                            mean_var(LM)
                    for t in range(TT):
                        dve.wait_ge(down_done, J * 2 + t // 2 + 1)
                        dve.scalar_tensor_tensor(xs[:, fs, t, :], Dn[t // 2][:, (t % 2) * D:(t % 2 + 1) * D],
                                                 kdown[:, 0:1], xs[:, fs, t, :], ALU.mult, ALU.add).then_inc(x_ffn, 1)


_INS = ['L0_attn_x', 'L0_attn_weight', 'L0_attn_bias', 'L0_attn_decay_value', 'L0_ffn_SU_ug', 'L0_ffn_SU_dp',
        'L0_ffn_Wscale_ug', 'L0_ffn_Wscale_dp', 'L0_ffn_W_up', 'L0_ffn_W_gate', 'L0_ffn_W_down']
_OUTS = [((16, 256, 256), 'float32')]


def kernel(**inputs):
    import numpy as _np
    import concourse.bacc as _bacc
    from concourse import mybir as _mybir
    from concourse.bass_utils import run_bass_kernel_spmd as _run

    nc = _bacc.Bacc("TRN2", target_bir_lowering=False, num_devices=1)
    arrays, args = {}, []
    for name in _INS:
        a = _np.ascontiguousarray(inputs[name])
        arrays[f"in_{name}_dram"] = a
        args.append(nc.dram_tensor(f"in_{name}_dram", a.shape, _mybir.dt.from_np(a.dtype), kind="ExternalInput").ap())
    for i, (shape, dtype) in enumerate(_OUTS):
        dt = _mybir.dt.from_np(_np.dtype(dtype))
        args.append(nc.dram_tensor(f"out_{i}_dram", shape, dt, kind="ExternalOutput").ap())
    macaron_kernel(nc, *args)
    r = _run(nc, [arrays], core_ids=[0])
    got = tuple(r.results[0][f"out_{i}_dram"] for i in range(len(_OUTS)))
    return got[0]
```
